# Optimizing a Trainium2 kernel written in Bass

```python
import numpy as np
import jax
import jax.numpy as jnp

def _softmax(x, axis=-1):
    return jax.nn.softmax(x, axis=axis)

def _gelu(x):
    return jax.nn.gelu(x, approximate=True)

def _silu(x):
    return jax.nn.silu(x)

def _sigmoid(x):
    return jax.nn.sigmoid(x)

def _layernorm(x, axis=-1, eps=1e-05):
    m = jnp.mean(x, axis=axis, keepdims=True)
    v = jnp.var(x, axis=axis, keepdims=True)
    return (x - m) / jnp.sqrt(v + eps)

def _scatter_add(tgt, idx, src, axis=0):
    return tgt.at[idx].add(src)

def _segment_sum(src, seg, n):
    return jax.ops.segment_sum(src, seg, n)
kernel_name = 'mk_adaln_ffn_d1_seqx_r8_a362b8'

def setup_inputs(seed: int=0):
    np.random.seed(seed)
    _w = jnp.asarray

    def _rec_inputs():
        import jax
        import jax.numpy as jnp
        _rk = jax.random.key(seed)
        x = -0.000125 + 0.9999 * jax.random.normal(jax.random.fold_in(_rk, 1), (128, 32, 256), jnp.float32)
        _lenS = 32 - jax.random.randint(jax.random.fold_in(_rk, 7), (128,), 0, max(1, 32 // 4) + 1, jnp.int32)
        _lenS2 = 32 - jax.random.randint(jax.random.fold_in(_rk, 8), (128,), 0, max(1, 32 // 4) + 1, jnp.int32)
        itok_B_0_7 = jax.random.randint(jax.random.fold_in(_rk, 11), (128,), 0, 8, jnp.int32)
        fside_8xS_0 = -0.00162727 + 0.0609077 * jax.random.normal(jax.random.fold_in(_rk, 12), (8, 32), jnp.float32)
        return (x, itok_B_0_7, fside_8xS_0)
    x, itok_B_0_7, fside_8xS_0 = _rec_inputs()

    def _L0_cond_setup():
        import jax, jax.numpy as jnp
        import numpy as np
        B, C, T = (64, 32, 256)
        D, N = (32, 8)
        key = jax.random.key(seed)
        k_x, k_s, k_w, k_b = jax.random.split(key, 4)
        scale = 1.0 / np.sqrt(C)
        x = jax.random.normal(k_x, (B, C, T), dtype=jnp.float32)
        subjects = jax.random.randint(k_s, (B,), 0, N, dtype=jnp.int64)
        weights = jax.random.normal(k_w, (N, C, D), dtype=jnp.float32) * scale
        bias = jax.random.normal(k_b, (N, D), dtype=jnp.float32) * scale
        return {'x': x, 'subjects': subjects, 'weights': weights, 'bias': bias}
    _L0_cond_all = _L0_cond_setup()
    _L0_cond_in = {k: v for k, v in _L0_cond_all.items() if k in ('weights',)}
    del _L0_cond_all

    def _L0_ffn_setup():
        import jax, jax.numpy as jnp
        import numpy as np
        B, T = (1, 64)
        DIM = 256
        MOE_INTER = 176
        N_EXPERTS = 64
        TOPK = 6
        N_SHARED = 2
        SHARED_INTER = N_SHARED * MOE_INTER
        CAPACITY = 128
        ROUTE_SCALE = 1.0
        key = jax.random.key(seed)
        ks = jax.random.split(key, 8)

        def w(k, shape, fan_in):
            return jax.random.normal(k, shape, jnp.float32) * fan_in ** (-0.5)
        return {'x': jax.random.normal(ks[0], (B, T, DIM), jnp.float32), 'gate_w': w(ks[1], (N_EXPERTS, DIM), DIM), 'w1': w(ks[2], (N_EXPERTS, MOE_INTER, DIM), DIM), 'w2': w(ks[3], (N_EXPERTS, DIM, MOE_INTER), MOE_INTER), 'w3': w(ks[4], (N_EXPERTS, MOE_INTER, DIM), DIM), 'sw1': w(ks[5], (SHARED_INTER, DIM), DIM), 'sw2': w(ks[6], (DIM, SHARED_INTER), SHARED_INTER), 'sw3': w(ks[7], (SHARED_INTER, DIM), DIM)}
    _L0_ffn_all = _L0_ffn_setup()
    _L0_ffn_in = {k: v for k, v in _L0_ffn_all.items() if k in ('gate_w', 'w1', 'w2', 'w3', 'sw1', 'sw2', 'sw3')}
    del _L0_ffn_all
    return {'x': x, 'itok_B_0_7': itok_B_0_7, 'fside_8xS_0': fside_8xS_0, 'L0_cond_weights': _L0_cond_in['weights'], 'L0_ffn_gate_w': _L0_ffn_in['gate_w'], 'L0_ffn_w1': _L0_ffn_in['w1'], 'L0_ffn_w2': _L0_ffn_in['w2'], 'L0_ffn_w3': _L0_ffn_in['w3'], 'L0_ffn_sw1': _L0_ffn_in['sw1'], 'L0_ffn_sw2': _L0_ffn_in['sw2'], 'L0_ffn_sw3': _L0_ffn_in['sw3']}

def reference(x, itok_B_0_7, fside_8xS_0, L0_cond_weights, L0_ffn_gate_w, L0_ffn_w1, L0_ffn_w2, L0_ffn_w3, L0_ffn_sw1, L0_ffn_sw2, L0_ffn_sw3):
    import jax
    import jax.numpy as jnp

    def _L0_cond_ref(x, subjects, weights, bias):
        import jax, jax.numpy as jnp
        import numpy as np
        B, C, T = (64, 32, 256)
        D, N = (32, 8)
        w = weights[subjects]
        b = bias[subjects]
        out = jnp.einsum('bct,bcd->bdt', x, w)
        out = out + b[:, :, None]
        return out

    def _L0_ffn_ref(x, gate_w, w1, w2, w3, sw1, sw2, sw3):
        import jax, jax.numpy as jnp
        import numpy as np
        B, T = (1, 64)
        DIM = 256
        MOE_INTER = 176
        N_EXPERTS = 64
        TOPK = 6
        N_SHARED = 2
        SHARED_INTER = N_SHARED * MOE_INTER
        CAPACITY = 128
        ROUTE_SCALE = 1.0
        Bb, Tt, D = x.shape
        xf = x.reshape(-1, D)
        N = xf.shape[0]
        logits = xf @ gate_w.T
        scores = jax.nn.softmax(logits, axis=-1)
        gate_vals, idx = jax.lax.top_k(scores, TOPK)
        gate_vals = gate_vals * ROUTE_SCALE
        E = gate_w.shape[0]
        fe = idx.reshape(-1)
        ft = jnp.repeat(jnp.arange(N), TOPK)
        onehot = (fe[:, None] == jnp.arange(E)[None, :]).astype(jnp.int32)
        pos = jnp.take_along_axis(jnp.cumsum(onehot, axis=0) - 1, fe[:, None], axis=1)[:, 0]
        keep = pos < CAPACITY
        buf = jnp.full((E, CAPACITY), N, dtype=jnp.int32)
        buf = buf.at[fe, pos].set(ft.astype(jnp.int32), mode='drop')
        xpad = jnp.concatenate([xf, jnp.zeros((1, D), xf.dtype)], axis=0)
        xe = xpad[buf]
        h = jax.nn.silu(jnp.einsum('ecd,eid->eci', xe, w1)) * jnp.einsum('ecd,eid->eci', xe, w3)
        ye = jnp.einsum('eci,edi->ecd', h, w2)
        pc = jnp.minimum(pos, CAPACITY - 1)
        op = ye[fe, pc] * keep[:, None].astype(ye.dtype)
        routed = (op * gate_vals.reshape(-1)[:, None]).reshape(N, TOPK, D).sum(axis=1)
        z = jax.nn.silu(xf @ sw1.T) * (xf @ sw3.T) @ sw2.T
        return (routed + z).reshape(Bb, Tt, D)
    x = x + _L0_ffn_ref(_L0_cond_ref(x, itok_B_0_7, L0_cond_weights, fside_8xS_0), L0_ffn_gate_w, L0_ffn_w1, L0_ffn_w2, L0_ffn_w3, L0_ffn_sw1, L0_ffn_sw2, L0_ffn_sw3)
    return x

_drawn_inputs = setup_inputs


def setup_inputs(seed=0):
    import zlib

    import numpy as np

    out = dict(_drawn_inputs(seed))
    spreads = {}
    factors = {}
    for name, (base, spread) in spreads.items():
        noise = np.random.default_rng([zlib.crc32(name.encode()), seed]).standard_normal(out[name].shape)
        drawn = base * np.exp(spread * noise) if base else spread * noise
        out[name] = jnp.asarray(drawn.astype(out[name].dtype))
    for name, factor in factors.items():
        out[name] = (out[name] * factor).astype(out[name].dtype)
    return out
```

```python
import numpy as np
import concourse.bass as bass
from concourse import mybir
from contextlib import ExitStack

F32, I32, BF16, F16 = mybir.dt.float32, mybir.dt.int32, mybir.dt.bfloat16, mybir.dt.float16
ACT, ALU, AX = mybir.ActivationFunctionType, mybir.AluOpType, mybir.AxisListType

B, C, T = 128, 32, 256
NSUB = 8
D = T
E, TOPK, INTER, CAP = 64, 6, 176, 128
SINTER = 2 * INTER
P = 128
N = B * C
NT = N // P
SPT = P // C
KD = D // P
GT = 4
NG = NT // GT
PEELED = 4
GTOK = GT * P
ROW = D + E
IH = INTER // 2
SCH = [(0, 128), (128, 128), (256, SINTER - 256)]
UNITS = 2 * len(SCH)
HTOK = GTOK // 2
EARLY = 5
SLOTS = 4
CW = C + 1
BIG = 3.0e38
GONE = -3.0e38
FLOOR = -87.3
UNCHOSEN = 64 * 128
HALF_N = N // 2


def wait(eng, sem, count):
    if not (isinstance(count, int) and count <= 0):
        eng.wait_ge(sem, count)


def wait_apart(eng, sem, count, passed):
    if not (isinstance(count, int) and count <= 0):
        eng.wait_ge(sem, count)
        eng.sem_inc(passed, 1)


def build_adaln_moe(nc, x, subj, table, gate_t, w13_t, w2_t, sw13_t, sw2_t, out):
    x_rows = x.rearrange("b c t -> (b c) t").rearrange("(i p) t -> p i t", p=P)
    out_rows = out.rearrange("b c t -> (b c) t").rearrange("(i p) t -> p i t", p=P)

    ctx = ExitStack()
    with ctx:
        def sb(name, shape, dt):
            return ctx.enter_context(nc.sbuf_tensor(name, shape, dt))

        def sem(name):
            return ctx.enter_context(nc.semaphore(name))

        wsel_dram = nc.dram_tensor("wsel_dram", (B, C, CW), F32).ap()
        rows_dram = nc.dram_tensor("rows_dram", (N, ROW), F32).ap()
        acc_dram = [nc.dram_tensor(f"acc{a}_dram", (N + CAP, D), F32).ap() for a in range(2)]
        wsel_tiles = wsel_dram.rearrange("(i j) c w -> (j c) i w", j=SPT)
        rows_tiles = rows_dram.rearrange("(i p) n -> p i n", p=P)
        acc_tiles = [a[0:N, :].rearrange("(i p) n -> p i n", p=P) for a in acc_dram]

        x_all = sb("x_all", [P, NT, D], F32)
        yT_all = sb("yT_all", [P, KD, N], F32)
        sw13 = sb("sw13", [P, KD, 2 * SINTER], F32)
        sw2 = sb("sw2", [P, len(SCH), D], F32)
        gate_sb = sb("gate_sb", [P, KD, E], F32)
        subj_sb = sb("subj_sb", [P, 1], I32)
        wsel = sb("wsel", [P, C * CW], F32)
        wcmp = sb("wcmp", [P, 2, GT, CW], F32)
        wblk = sb("wblk", [P, 2, GT, P], F32)
        blocks = sb("blocks", [P, SPT, C], F32)
        yrow = sb("yrow", [P, 2, GT, D], F32)
        ytr = sb("ytr", [P, GT, KD, P], F32)
        key = sb("key", [P, 2, GT, E + 2], F32)
        left = sb("left", [P, GT, E + 2], F32)
        rowmax = sb("rowmax", [P, GT], F32)
        top8 = sb("top8", [P, GT, 8], F32)
        chosen = sb("chosen", [P, NT, E], BF16)
        pair = sb("pair", [P, 2, E], F32)
        gsum = sb("gsum", [P, E], F32)
        carry = sb("carry", [P, NG + 1, E], BF16)
        exps = sb("exps", [P, 2, GT, E], F32)
        esum = sb("esum", [P, GT], F32)
        rsum = sb("rsum", [P, 2, GT], F32)
        scores = sb("scores", [P, 2, GT, E], F32)
        slot1 = sb("slot1", [P, GT, E], F32)
        slotv = sb("slotv", [P, GT, E], F32)
        s8 = sb("s8", [P, GT, 8], F32)
        slot_i = sb("slot_i", [P, GT, 8], I32)
        pos_i = sb("pos_i", [P, GT, 8], I32)
        exp_i = sb("exp_i", [P, GT, 8], I32)
        pos_h = sb("pos_h", [P, GT, 8], F16)
        exp_h = sb("exp_h", [P, GT, 8], F16)
        onepos = sb("onepos", [P, 2, GT, P, TOPK], F16)
        oneexp = sb("oneexp", [P, 2, GT, E, TOPK], F16)
        payload = sb("payload", [P, 2, GT, E, TOPK], F16)
        idxf = sb("idxf", [P, E], F32)
        empty = sb("empty", [P, E], F32)
        idx_read = sb("idx_read", [P, E], I32)
        idx_write = sb("idx_write", [P, E], I32)
        sg = sb("sg", [P, 3, HTOK], F32)
        hT = sb("hT", [P, len(SCH), GTOK], F32)
        w13 = sb("w13", [P, SLOTS, KD, 2 * INTER], F32)
        w2 = sb("w2", [IH, SLOTS, 2, D], F32)
        ri = sb("ri", [P, SLOTS, 1], I32)
        wi = sb("wi", [P, SLOTS, 1], I32)
        xe = sb("xe", [P, SLOTS, ROW], F32)
        xeT = sb("xeT", [P, 2, KD, P], F32)
        eg = sb("eg", [P, 2, INTER], F32)
        eh = sb("eh", [P, 2, INTER], F32)
        ehT = sb("ehT", [IH, 2, 2, P], F32)
        ey = sb("ey", [P, SLOTS, D], F32)
        acc_sb = [sb(f"acc{a}_sb", [P, 2, GT, D], F32) for a in range(2)]
        ident = sb("ident", [P, P], F32)
        earlier = sb("earlier", [P, P], BF16)
        mark = sb("mark", [P, P], BF16)
        ones = sb("ones", [P, P], BF16)
        zeros_h = sb("zeros_h", [P, P], F16)
        zeros = sb("zeros", [P, 1024], F32)
        iota_p = sb("iota_p", [P, 1], F32)
        ids_i = sb("ids_i", [P, NT], I32)
        ids = sb("ids", [P, NT], F32)
        dump_p = sb("dump_p", [P, 1], F32)
        slot0 = sb("slot0", [P, E], F32)
        iota_c = sb("iota_c", [P, P, TOPK], F16)
        iota_e = sb("iota_e", [P, E, TOPK], F16)

        bank = [ctx.enter_context(nc.psum_tensor(f"bank{i}", [P, 512], F32)) for i in range(8)]

        y_ps = [bank[4 + q // 2][:, (q % 2) * D:(q % 2) * D + D] for q in range(GT)]
        yT_ps = [bank[h][:, :].rearrange("p (q k c) -> p q k c", q=2, k=KD) for h in range(2)]
        lg_ps = [bank[2 + par][:, 0:GT * E].rearrange("p (q e) -> p q e", q=GT) for par in range(2)]
        unit_ps = [bank[i][:, :].rearrange("p (w t) -> p w t", w=2) for i in range(3)]
        z_ps = [bank[4 + h][:, :].rearrange("p (q n) -> p q n", q=2) for h in range(2)]
        pos_ps = bank[6][:, 0:GT * E].rearrange("p (q e) -> p q e", q=GT)
        cnt_ps = bank[6][:, 0:E]
        tab_ps = bank[7][:, 0:E]
        xeT_ps = [bank[0 + i][:, 0:D].rearrange("p (k c) -> p k c", k=KD) for i in range(2)]
        h_ps = [bank[2 + i][:, 0:2 * INTER] for i in range(2)]
        ehT_ps = [bank[4 + i][0:IH, 0:2 * P].rearrange("p (k c) -> p k c", k=2) for i in range(2)]
        ey_ps = [bank[6 + i][:, 0:D] for i in range(2)]

        s = {}
        for name in (
            "pool_const", "dve_passed", "pool_passed", "sp_passed", "block_zero", "block_one", "dve_const", "consts", "subj_in", "table_out", "wsel_out", "gate_in", "sw_in",
            "wblk_done", "y_done", "yrow_done", "yT_done", "ytr_done", "ycopy_done", "lg_done",
            "rowmax_done", "shift_done", "key_done", "top8_done", "left_done", "chosen_done", "pair_done", "gsum_done",
            "carry_done", "exp_done", "esum_done", "recip_done", "score_done",
            "pos_done", "slot1_done", "slotv_done", "s8_done", "sloti_done", "split_done", "code_done",
            "onepos_done", "oneexp_done", "payload_done", "tab_done", "tab_final", "idxf_done", "empty_done", "idx_done",
            "unit_done", "silu_done", "hT_done", "z_done", "zadd_done",
            "acc_zero", "ri_done", "wi_done", "xt_done", "xeT_done", "h_done", "eg_done", "eh_done",
            "eht_done", "ehT_done", "ey_done", "eyrow_done",
            "addA_done", "addB_done", "out_pool", "out_sp",
        ):
            s[name] = sem(name)
        x_in = [sem(f"x_in{i}") for i in range(2)]
        wcmp_in = [sem(f"wcmp_in{i}") for i in range(2)]
        y_stored = [sem(f"y_stored{i}") for i in range(2)]
        p_stored = [sem(f"p_stored{i}") for i in range(2)]
        w_in = [sem(f"w_in{i}") for i in range(SLOTS)]
        xe_in = [sem(f"xe_in{i}") for i in range(SLOTS)]
        acc_added = [sem(f"acc_added{i}") for i in range(2)]
        acc_in = [sem(f"acc_in{i}") for i in range(2)]

        block = ctx.enter_context(nc.Block())

        def over_groups(eng, step):
            for g in range(PEELED):
                step(g, g % 2, g // 2)
            with eng.Fori(PEELED // 2, NG // 2) as it:
                for par in range(2):
                    step(it * 2 + par, par, it)

        def landed(e, slot):
            if isinstance(e, int):
                return ((e - SLOTS) // 2 + 1) * 16 if e >= SLOTS else 0
            return e * 8 - (SLOTS + slot % 2) * 8 + 16

        LATE = list(range(EARLY, NG))
        BETWEEN = {(5, 2): 0, (5, 4): 5, (5, 5): 1, (6, 1): 6, (6, 3): 2, (6, 5): 3, (7, 1): 7, (7, 3): 4}
        ORDER = list(BETWEEN.values())

        @block.sync
        def _(sp):
            sp.dma_start(subj_sb[:, :], subj).then_inc(s["subj_in"], 16)

            def load_group(g, par, rounds):
                wait(sp, x_in[par], rounds * 16)
                sp.dma_start(x_all[:, bass.ds(g * GT, GT), :], x_rows[:, bass.ds(g * GT, GT), :]).then_inc(x_in[par], 16)

            def load_weights(g, par, rounds):
                wait_apart(sp, s["wblk_done"], g - 1, s["sp_passed"])
                wait_apart(sp, s["yrow_done"], (g - 1) * GT, s["sp_passed"])
                sp.dma_start(wcmp[:, par, :, :], wsel_tiles[:, bass.ds(g * GT, GT), :]).then_inc(wcmp_in[par], 16)

            def store_rows(g, par):
                sp.wait_ge(s["yrow_done"], g * GT + GT)
                sp.dma_start(rows_tiles[:, bass.ds(g * GT, GT), 0:D], yrow[:, par, :, :]).then_inc(y_stored[par], 16)

            def store_scores(g, par):
                sp.wait_ge(s["score_done"], g + 1)
                sp.dma_start(rows_tiles[:, bass.ds(g * GT, GT), D:ROW], scores[:, par, :, :]).then_inc(p_stored[par], 16)

            load_group(0, 0, 0)
            load_group(1, 1, 0)
            sp.dma_start(gate_sb[:, :, :], gate_t).then_inc(s["gate_in"], 16)
            sp.dma_start(sw13[:, :, :], sw13_t).then_inc(s["sw_in"], 16)
            sp.dma_start(sw2[:, 0:2, :], sw2_t[0:2 * P, :].rearrange("(m p) n -> p m n", p=P)).then_inc(s["sw_in"], 16)
            sp.dma_start(sw2[0:SCH[2][1], 2, :], sw2_t[2 * P:SINTER, :]).then_inc(s["sw_in"], 16)
            sp.wait_ge(s["wsel_out"], 16)
            load_weights(0, 0, 0)
            load_weights(1, 1, 0)

            def turn(g, par, rounds):
                if not (isinstance(g, int) and g < 2):
                    store_scores(g - 2, par)
                store_rows(g, par)
                load_group(g + 2, par, rounds + 1)
                load_weights(g + 2, par, rounds + 1)

            for g in range(PEELED):
                turn(g, g % 2, g // 2)
            with sp.Fori(PEELED // 2, NG // 2 - 1) as it:
                for par in range(2):
                    turn(it * 2 + par, par, it)
            for g in range(NG - 2, NG):
                store_scores(g - 2, g % 2)
                store_rows(g, g % 2)
            for g in range(NG - 2, NG):
                store_scores(g, g % 2)

            def load_expert(e, slot):
                wait(sp, s["ey_done"], e - SLOTS + 1)
                sp.dma_start(w13[:, slot, :, :], w13_t[bass.ds(e, 1)].rearrange("a p k n -> p (a k) n")).then_inc(w_in[slot], 16)
                sp.dma_start(w2[:, slot, :, :], w2_t[bass.ds(e, 1)].rearrange("a p k n -> p (a k) n")).then_inc(w_in[slot], 16)

            for slot in range(SLOTS):
                load_expert(slot, slot)
            per = zeros.shape[1] // D
            for a in range(2):
                flat = acc_dram[a][0:N, :].rearrange("(r p n) d -> r p (n d)", p=P, n=per)
                for r in range(N // P // per):
                    sp.dma_start(flat[r], zeros[:, :]).then_inc(s["acc_zero"], 16)
                sp.dma_start(acc_dram[a][N:N + CAP, :], zeros[:, 0:D]).then_inc(s["acc_zero"], 16)
            with sp.Fori(1, E // SLOTS) as it:
                for slot in range(SLOTS):
                    load_expert(it * SLOTS + slot, slot)

            for a in range(2):
                sp.wait_ge(acc_added[a], E // 2 * 16)
            for n, g in enumerate(ORDER):
                wait(sp, s["addB_done"], n - 1)
                for a in range(2):
                    sp.dma_start(acc_sb[a][:, n % 2, :, :], acc_tiles[a][:, g * GT:(g + 1) * GT, :]).then_inc(acc_in[n % 2], 16)
            for h in range(2):
                sp.wait_ge(s["zadd_done"], (NG - 1) * 2 + h + 1)
                i = (NG - 1) * GT + 2 * h
                sp.dma_start(out_rows[:, i:i + 2, :], x_all[:, i:i + 2, :]).then_inc(s["out_sp"], 16)
            sp.wait_ge(s["out_sp"], 2 * 16)

        @block.gpsimd
        def _(pool):
            pool.wait_ge(s["subj_in"], 16)
            pool.indirect_dma_start(wsel[:, :], None, table, bass.IndirectOffsetOnAxis(subj_sb[:, 0:1], 0),
                                    bounds_check=NSUB - 1, oob_is_err=False).then_inc(s["table_out"], 16)
            nc.gpsimd.memset(ident[:, :], 1.0)
            nc.gpsimd.memset(earlier[:, :], 1.0)
            nc.gpsimd.memset(mark[:, :], -float(UNCHOSEN))
            nc.gpsimd.memset(ones[:, :], 1.0)
            nc.gpsimd.memset(zeros_h[:, :], 0.0)
            nc.gpsimd.memset(zeros[:, :], 0.0)
            nc.gpsimd.memset(carry[:, 0, :], 0.0)
            nc.gpsimd.memset(key[:, :, :, E:E + 2], BIG).then_inc(s["pool_const"], 1)
            pool.wait_ge(s["table_out"], 16)
            pool.dma_start(wsel_dram.rearrange("b c w -> b (c w)"), wsel[:, :]).then_inc(s["wsel_out"], 16)
            pool.wait_ge(s["pool_const"], 1)
            nc.gpsimd.affine_select(out=ident[:, :], in_=ident[:, :], compare_op=ALU.is_equal, fill=0.0,
                                    base=0, pattern=[[-1, P]], channel_multiplier=1)
            nc.gpsimd.affine_select(out=mark[:, :], in_=mark[:, :], compare_op=ALU.is_equal, fill=0.0,
                                    base=0, pattern=[[-1, P]], channel_multiplier=1)
            nc.gpsimd.affine_select(out=earlier[:, :], in_=earlier[:, :], compare_op=ALU.is_gt, fill=0.0,
                                    base=0, pattern=[[1, P]], channel_multiplier=-1)
            nc.gpsimd.iota(iota_p[:, :], [[1, 1]], base=0, channel_multiplier=1, allow_small_or_imprecise_dtypes=True)
            nc.gpsimd.iota(dump_p[:, :], [[1, 1]], base=HALF_N, channel_multiplier=1, allow_small_or_imprecise_dtypes=True)
            nc.gpsimd.iota(ids_i[:, :], [[P, NT]], base=-HALF_N, channel_multiplier=1)
            nc.gpsimd.iota(slot0[:, :], [[CAP, E]], base=UNCHOSEN + 1, channel_multiplier=0,
                           allow_small_or_imprecise_dtypes=True)
            nc.gpsimd.iota(iota_c[:, :, :], [[1, P], [0, TOPK]], base=0, channel_multiplier=0,
                           allow_small_or_imprecise_dtypes=True)
            nc.gpsimd.iota(iota_e[:, :, :], [[1, E], [0, TOPK]], base=0, channel_multiplier=0,
                           allow_small_or_imprecise_dtypes=True).then_inc(s["consts"], 1)

            def blocks_of(g, par, rounds):
                pool.wait_ge(wcmp_in[par], (rounds + 1) * 16)
                wait(pool, s["y_done"], (g - 1) * 2)
                nc.gpsimd.tensor_tensor(wblk[:, par, :, :].rearrange("p q (j d) -> p q j d", j=SPT),
                                        wcmp[:, par, :, 0:C].unsqueeze(2).to_broadcast([P, GT, SPT, C]),
                                        blocks[:, :, :].unsqueeze(1).to_broadcast([P, GT, SPT, C]),
                                        ALU.mult).then_inc(s["wblk_done"], 1)

            def carry_of(g):
                pool.wait_ge(s["chosen_done"], g + 1)
                wait(pool, s["carry_done"], g)
                nc.gpsimd.tensor_tensor(pair[:, :, :], chosen[:, bass.ds(g * GT, 2), :], chosen[:, bass.ds(g * GT + 2, 2), :],
                                        ALU.add).then_inc(s["pair_done"], 1)
                pool.wait_ge(s["pair_done"], g + 1)
                nc.gpsimd.tensor_tensor(gsum[:, :], pair[:, 0, :], pair[:, 1, :], ALU.add).then_inc(s["gsum_done"], 1)
                pool.wait_ge(s["gsum_done"], g + 1)
                nc.gpsimd.tensor_tensor(carry[:, bass.ds(g + 1, 1), :].rearrange("p a e -> p (a e)"),
                                        carry[:, bass.ds(g, 1), :].rearrange("p a e -> p (a e)"),
                                        gsum[:, :], ALU.add).then_inc(s["carry_done"], 1)

            def scores_of(g, par, rounds):
                pool.wait_ge(s["recip_done"], g + 1)
                wait(pool, p_stored[par], rounds * 16)
                nc.gpsimd.tensor_tensor(scores[:, par, :, :], exps[:, par, :, :],
                                        rsum[:, par, :].unsqueeze(2).to_broadcast([P, GT, E]),
                                        ALU.mult).then_inc(s["score_done"], 1)

            pool.wait_ge(s["consts"], 1)
            pool.wait_ge(s["block_one"], 1)
            def turn(g, par, rounds):
                blocks_of(g, par, rounds)
                if not (isinstance(g, int) and g < 2):
                    scores_of(g - 2, par, rounds - 1)
                    carry_of(g - 2)

            over_groups(pool, turn)
            for g in range(NG - 2, NG):
                scores_of(g, g % 2, NG // 2 - 1)
                carry_of(g)

            for par in range(2):
                pool.wait_ge(y_stored[par], NG // 2 * 16)
                pool.wait_ge(p_stored[par], NG // 2 * 16)
            pool.wait_ge(s["idx_done"], 1)

            def gather(e, slot, rounds):
                if rounds is not None:
                    pool.wait_ge(s["xt_done"], e - SLOTS + 1)
                    pool.wait_ge(s["eh_done"], e - SLOTS + 1)
                wait_apart(pool, s["ri_done"], e + 1, s["pool_passed"])
                pool.indirect_dma_start(xe[:, slot, :], None, rows_dram, bass.IndirectOffsetOnAxis(ri[:, slot, 0:1], 0),
                                        bounds_check=N - 1, oob_is_err=False).then_inc(xe_in[slot], 16)

            def scatter(e, slot):
                a = slot % 2
                wait(pool, acc_added[a], (e - slot) // 2 * 16 + slot // 2 * 16 if isinstance(e, int) else e * 8 - a * 8)
                wait_apart(pool, s["wi_done"], e + 1, s["pool_passed"])
                wait_apart(pool, s["eyrow_done"], e + 1, s["pool_passed"])
                pool.indirect_dma_start(acc_dram[a], bass.IndirectOffsetOnAxis(wi[:, slot, 0:1], 0), ey[:, slot, :], None,
                                        bounds_check=N + CAP - 1, oob_is_err=True, compute_op=ALU.add).then_inc(acc_added[a], 16)

            for slot in range(SLOTS):
                gather(slot, slot, None)
            pool.wait_ge(s["acc_zero"], 2 * (N // P // (zeros.shape[1] // D) + 1) * 16)
            for slot in range(SLOTS):
                gather(SLOTS + slot, slot, 1)
                scatter(slot, slot)
            with pool.Fori(1, E // SLOTS - 1) as it:
                for slot in range(SLOTS):
                    gather(it * SLOTS + (SLOTS + slot), slot, it + 1)
                    scatter(it * SLOTS + slot, slot)
            for slot in range(SLOTS):
                scatter(E - SLOTS + slot, slot)

            for g in (0, 1, 5, 2, 3, 6, 4):
                if g < EARLY:
                    pool.wait_ge(s["addB_done"], ORDER.index(g) + 1)
                else:
                    pool.wait_ge(s["zadd_done"], (g + 1) * 2)
                pool.dma_start(out_rows[:, g * GT:(g + 1) * GT, :], x_all[:, g * GT:(g + 1) * GT, :]).then_inc(s["out_pool"], 16)
            pool.wait_ge(s["out_pool"], (NG - 1) * 16)

        @block.scalar
        def _(act):
            def exp_of(g, par):
                act.wait_ge(s["key_done"], g + 1)
                wait(act, s["score_done"], g - 1)
                nc.scalar.activation(exps[:, par, :, :], key[:, par, :, 0:E], ACT.Exp).then_inc(s["exp_done"], 1)

            def step(g, par, rounds):
                act.wait_ge(wcmp_in[par], (rounds + 1) * 16)
                wait(act, y_stored[par], rounds * 16)
                for q in range(GT):
                    act.wait_ge(s["y_done"], g * 2 + q // 2 + 1)
                    nc.scalar.activation(yrow[:, par, q, :], y_ps[q], ACT.Identity,
                                         bias=wcmp[:, par, q, C:CW]).then_inc(s["yrow_done"], 1)
                if not (isinstance(g, int) and g == 0):
                    exp_of(g - 1, 1 - par)
                wait(act, s["lg_done"], g)
                wait(act, s["ycopy_done"], g)
                for h in range(2):
                    act.wait_ge(s["yT_done"], g * 2 + h + 1)
                    nc.scalar.copy(ytr[:, 2 * h:2 * h + 2, :, :], yT_ps[h]).then_inc(s["ytr_done"], 1)

            over_groups(act, step)
            exp_of(NG - 1, 1)

            def silu(g, u):
                m = SCH[u // 2][1]
                act.wait_ge(s["unit_done"], g * UNITS + u + 1)
                wait(act, s["hT_done"], g * UNITS + u - 2)
                nc.scalar.activation(sg[0:m, u % 3, :], unit_ps[u % 3][0:m, 0, :], ACT.Silu).then_inc(s["silu_done"], 1)

            def pay(r, par):
                act.wait_ge(s["oneexp_done"], r + 1)
                wait(act, s["tab_done"], r - 1)
                for q in range(GT):
                    last = nc.scalar.activation(payload[:, par, q, :, :], oneexp[:, par, q, :, :], ACT.Copy,
                                                scale=ids[:, bass.ds(r * GT + q, 1)])
                last.then_inc(s["payload_done"], 1)

            def early(g):
                for half in range(2):
                    for u in range(3):
                        silu(g, 3 * half + u)
                    pay(g * 2 + half, half)

            early(0)
            with act.Fori(1, EARLY - 1) as g:
                early(g)
            for u in range(UNITS):
                silu(EARLY - 1, u)

            def take_xT(e, slot):
                act.wait_ge(s["xt_done"], e + 1)
                wait(act, s["h_done"], e - 1)
                nc.scalar.copy(xeT[:, slot % 2, :, :], xeT_ps[slot % 2]).then_inc(s["xeT_done"], 1)

            def take_h(e, slot):
                act.wait_ge(s["h_done"], e + 1)
                wait(act, s["eh_done"], e - 1)
                nc.scalar.activation(eg[:, slot % 2, :], h_ps[slot % 2][:, 0:INTER], ACT.Silu).then_inc(s["eg_done"], 1)

            def take_y(e, slot):
                act.wait_ge(s["ey_done"], e + 1)
                wait(act, acc_added[slot % 2], landed(e, slot))
                nc.scalar.copy(ey[:, slot, :], ey_ps[slot % 2]).then_inc(s["eyrow_done"], 1)

            def steady(e, slot):
                take_xT(e + 1, slot + 1)
                take_h(e, slot)
                take_y(e - 1, (slot - 1) % SLOTS)

            take_xT(0, 0)
            take_xT(1, 1)
            take_h(0, 0)
            for e in range(1, 1 + SLOTS):
                steady(e, e % SLOTS)
            with act.Fori(1, (E - SLOTS) // SLOTS) as it:
                for j in range(SLOTS):
                    steady(it * SLOTS + (1 + j), (1 + j) % SLOTS)
            for e in range(E - SLOTS + 1, E - 1):
                steady(e, e % SLOTS)
            take_h(E - 1, (E - 1) % SLOTS)
            take_y(E - 2, (E - 2) % SLOTS)
            take_y(E - 1, (E - 1) % SLOTS)

            for g in LATE:
                for u in range(UNITS):
                    silu(g, u)

        @block.vector
        def _(dve):
            nc.vector.memset(blocks[:, :, :], 0.0).then_inc(s["block_zero"], 1)
            dve.wait_ge(s["block_zero"], 1)
            for j in range(SPT):
                last = nc.vector.memset(blocks[j * C:(j + 1) * C, j, :], 1.0)
            last.then_inc(s["block_one"], 1)
            dve.wait_ge(s["consts"], 1)
            nc.vector.tensor_copy(ids[:, :], ids_i[:, :]).then_inc(s["dve_const"], 1)

            def choose(g, par):
                lg = lg_ps[par]
                dve.wait_ge(s["lg_done"], g + 1)
                nc.vector.tensor_reduce(rowmax[:, :], lg, AX.X, ALU.max).then_inc(s["rowmax_done"], 1)
                dve.wait_ge(s["rowmax_done"], g + 1)
                wait(dve, s["exp_done"], g - 1)
                k64 = key[:, par, :, 0:E]
                nc.vector.tensor_tensor(k64, lg, rowmax[:, :].unsqueeze(2).to_broadcast([P, GT, E]),
                                        ALU.subtract).then_inc(s["shift_done"], 1)
                dve.wait_ge(s["shift_done"], g + 1)
                nc.vector.tensor_scalar(k64, k64, FLOOR, None, ALU.max).then_inc(s["key_done"], 1)
                wait_apart(dve, s["key_done"], g + 1, s["dve_passed"])
                for q in range(GT):
                    last = nc.vector.max(top8[:, q, :], key[:, par, q, :])
                last.then_inc(s["top8_done"], 1)
                wait_apart(dve, s["top8_done"], g + 1, s["dve_passed"])
                for q in range(GT):
                    last = nc.vector.match_replace(left[:, q, :], top8[:, q, :], key[:, par, q, :], GONE)
                last.then_inc(s["left_done"], 1)
                dve.wait_ge(s["left_done"], g + 1)
                mine = chosen[:, bass.ds(g * GT, GT), :]
                nc.vector.tensor_tensor(mine, left[:, :, 0:E], k64, ALU.is_lt).then_inc(s["chosen_done"], 1)
                dve.wait_ge(s["exp_done"], g + 1)
                nc.vector.tensor_reduce(esum[:, :], exps[:, par, :, :], AX.X, ALU.add).then_inc(s["esum_done"], 1)
                dve.wait_ge(s["esum_done"], g + 1)
                wait(dve, s["score_done"], g - 1)
                nc.vector.reciprocal(rsum[:, par, :], esum[:, :]).then_inc(s["recip_done"], 1)

            def copy_yT(g):
                wait(dve, s["ytr_done"], g * 2 + 2)
                for k in range(KD):
                    last = nc.vector.tensor_copy(
                        yT_all[:, k, bass.ds(g * GTOK, GTOK)].rearrange("p (q c) -> p q c", q=GT), ytr[:, :, k, :])
                last.then_inc(s["ycopy_done"], 1)

            def turn(g, par, rounds):
                copy_yT(g)
                choose(g, par)

            over_groups(dve, turn)

            def slots_of(r, par):
                dve.wait_ge(s["pos_done"], r + 1)
                nc.vector.tensor_tensor(slot1[:, :, :], pos_ps, slot0[:, :].unsqueeze(1).to_broadcast([P, GT, E]),
                                        ALU.add).then_inc(s["slot1_done"], 1)
                dve.wait_ge(s["slot1_done"], r + 1)
                nc.vector.scalar_tensor_tensor(slotv[:, :, :], pos_ps, float(CAP - UNCHOSEN), slot1[:, :, :],
                                               ALU.is_lt, ALU.mult).then_inc(s["slotv_done"], 1)
                wait_apart(dve, s["slotv_done"], r + 1, s["dve_passed"])
                for q in range(GT):
                    last = nc.vector.max(s8[:, q, :], slotv[:, q, :])
                last.then_inc(s["s8_done"], 1)
                dve.wait_ge(s["s8_done"], r + 1)
                nc.vector.tensor_scalar(slot_i[:, :, :], s8[:, :, :], -1.0, None, ALU.add).then_inc(s["sloti_done"], 1)
                dve.wait_ge(s["sloti_done"], r + 1)
                nc.vector.tensor_scalar(pos_i[:, :, :], slot_i[:, :, :], CAP - 1, None, ALU.bitwise_and)
                nc.vector.tensor_scalar(exp_i[:, :, :], slot_i[:, :, :], 7, None, ALU.arith_shift_right).then_inc(s["split_done"], 1)
                dve.wait_ge(s["split_done"], r + 1)
                nc.vector.tensor_copy(pos_h[:, :, :], pos_i[:, :, :])
                nc.vector.tensor_copy(exp_h[:, :, :], exp_i[:, :, :]).then_inc(s["code_done"], 1)

            def one_hot_pos(r, par):
                dve.wait_ge(s["code_done"], r + 1)
                wait(dve, s["tab_done"], r - 1)
                for q in range(GT):
                    last = nc.vector.tensor_tensor(onepos[:, par, q, :, :], iota_c[:, :, :],
                                            pos_h[:, q, 0:TOPK].unsqueeze(1).to_broadcast([P, P, TOPK]),
                                            ALU.is_equal)
                last.then_inc(s["onepos_done"], 1)

            def one_hot_exp(r, par):
                wait(dve, s["payload_done"], r - 1)
                for q in range(GT):
                    last = nc.vector.tensor_tensor(oneexp[:, par, q, :, :], iota_e[:, :, :],
                                            exp_h[:, q, 0:TOPK].unsqueeze(1).to_broadcast([P, E, TOPK]),
                                            ALU.is_equal)
                last.then_inc(s["oneexp_done"], 1)

            def gated(g, u):
                m = SCH[u // 2][1]
                half = u % 2
                dve.wait_ge(s["silu_done"], g * UNITS + u + 1)
                wait(dve, s["z_done"], g * 2)
                nc.vector.tensor_tensor(hT[0:m, u // 2, half * HTOK:(half + 1) * HTOK], sg[0:m, u % 3, :],
                                        unit_ps[u % 3][0:m, 1, :], ALU.mult).then_inc(s["hT_done"], 1)

            def add_shared(g):
                for h in range(2):
                    dve.wait_ge(s["z_done"], g * 2 + h + 1)
                    xh = x_all[:, bass.ds(g * GT + 2 * h, 2), :]
                    nc.vector.tensor_tensor(xh, xh, z_ps[h], ALU.add).then_inc(s["zadd_done"], 1)

            def early(g):
                slots_of(g * 2, 0)
                gated(g, 0)
                one_hot_pos(g * 2, 0)
                gated(g, 1)
                one_hot_exp(g * 2, 0)
                gated(g, 2)
                slots_of(g * 2 + 1, 1)
                gated(g, 3)
                one_hot_pos(g * 2 + 1, 1)
                gated(g, 4)
                one_hot_exp(g * 2 + 1, 1)
                gated(g, 5)
                add_shared(g)

            early(0)
            with dve.Fori(1, EARLY - 1) as g:
                early(g)
            dve.wait_ge(s["tab_final"], 1)
            nc.vector.tensor_scalar(idxf[:, :], tab_ps, float(HALF_N), None, ALU.add).then_inc(s["idxf_done"], 1)
            nc.vector.tensor_scalar(empty[:, :], cnt_ps, iota_p[:, 0:1], dump_p[:, 0:1], ALU.is_le, ALU.mult).then_inc(s["empty_done"], 1)
            dve.wait_ge(s["idxf_done"], 1)
            nc.vector.tensor_copy(idx_read[:, :], idxf[:, :])
            dve.wait_ge(s["empty_done"], 1)
            nc.vector.tensor_tensor(idx_write[:, :], empty[:, :], idxf[:, :], ALU.add).then_inc(s["idx_done"], 1)
            for u in range(UNITS):
                gated(EARLY - 1, u)
            add_shared(EARLY - 1)

            def read_index(e, slot, rounds):
                wait(dve, xe_in[slot], rounds * 16)
                nc.vector.tensor_copy(ri[:, slot, :], idx_read[:, bass.ds(e, 1)]).then_inc(s["ri_done"], 1)

            def write_index(e, slot):
                wait(dve, acc_added[slot % 2], landed(e, slot))
                nc.vector.tensor_copy(wi[:, slot, :], idx_write[:, bass.ds(e, 1)]).then_inc(s["wi_done"], 1)

            def score_h(e, slot):
                dve.wait_ge(s["eg_done"], e + 1)
                wait(dve, s["eht_done"], e - 1)
                nc.vector.scalar_tensor_tensor(eh[:, slot % 2, :], eg[:, slot % 2, :], xe[:, slot, bass.ds(e + D, 1)],
                                               h_ps[slot % 2][:, INTER:2 * INTER], ALU.mult, ALU.mult).then_inc(s["eh_done"], 1)

            def take_hT(e, slot):
                dve.wait_ge(s["eht_done"], e + 1)
                wait(dve, s["ey_done"], e - 1)
                nc.vector.tensor_copy(ehT[:, slot % 2, :, :], ehT_ps[slot % 2]).then_inc(s["ehT_done"], 1)

            def steady(e, slot, rounds, more=True):
                take_hT(e - 1, (slot - 1) % SLOTS)
                write_index(e, slot)
                score_h(e, slot)
                if more:
                    read_index(e + SLOTS, slot, rounds + 1)

            for e in range(SLOTS):
                read_index(e, e, 0)
            write_index(0, 0)
            score_h(0, 0)
            read_index(SLOTS, 0, 1)
            for e in range(1, 1 + SLOTS):
                steady(e, e % SLOTS, e // SLOTS)
            with dve.Fori(1, (E - SLOTS) // SLOTS - 1) as it:
                for j in range(SLOTS):
                    e = 1 + j
                    steady(it * SLOTS + e, e % SLOTS, it + e // SLOTS)
            for e in range(E - 2 * SLOTS + 1, E):
                steady(e, e % SLOTS, e // SLOTS, e < E - SLOTS)
            take_hT(E - 1, (E - 1) % SLOTS)

            def combine(g):
                n = ORDER.index(g)
                mine = x_all[:, g * GT:(g + 1) * GT, :]
                dve.wait_ge(acc_in[n % 2], (n // 2 + 1) * 32)
                nc.vector.tensor_tensor(mine, mine, acc_sb[0][:, n % 2, :, :], ALU.add).then_inc(s["addA_done"], 1)
                dve.wait_ge(s["addA_done"], n + 1)
                nc.vector.tensor_tensor(mine, mine, acc_sb[1][:, n % 2, :, :], ALU.add).then_inc(s["addB_done"], 1)

            for g in LATE:
                for u in range(UNITS):
                    gated(g, u)
                    if (g, u) in BETWEEN:
                        combine(BETWEEN[g, u])
                dve.wait_ge(s["addB_done"], ORDER.index(g) + 1)
                add_shared(g)

        @block.tensor
        def _(pe):
            mm = nc.tensor.matmul
            pe.wait_ge(s["consts"], 1)
            mm(tab_ps, zeros_h[:, :], zeros_h[:, 0:E], start=True, stop=False)

            def logits(g, par):
                wait(pe, s["shift_done"], g - 1)
                for q in range(GT):
                    pe.wait_ge(s["ytr_done"], g * 2 + q // 2 + 1)
                    for k in range(KD):
                        last = mm(lg_ps[par][:, q, :], ytr[:, q, k, :], gate_sb[:, k, :], start=(k == 0), stop=(k == KD - 1))
                last.then_inc(s["lg_done"], 1)

            def step(g, par, rounds):
                pe.wait_ge(s["wblk_done"], g + 1)
                pe.wait_ge(x_in[par], (rounds + 1) * 16)
                for h in range(2):
                    wait(pe, s["yrow_done"], g * GT + 2 * h - 2)
                    for q in range(2 * h, 2 * h + 2):
                        last = mm(y_ps[q], wblk[:, par, q, :], x_all[:, bass.ds(g * GT + q, 1), :].rearrange("p a n -> p (a n)"),
                                  start=True, stop=True)
                    last.then_inc(s["y_done"], 1)
                if not (isinstance(g, int) and g == 0):
                    logits(g - 1, 1 - par)
                for h in range(2):
                    pe.wait_ge(s["yrow_done"], g * GT + 2 * h + 2)
                    wait(pe, s["ytr_done"], g * 2 + h - 1)
                    for q in range(2):
                        for k in range(KD):
                            last = nc.tensor.transpose(yT_ps[h][:, q, k, :], yrow[:, par, 2 * h + q, k * P:(k + 1) * P], ident[:, :])
                    last.then_inc(s["yT_done"], 1)

            pe.wait_ge(s["gate_in"], 16)
            over_groups(pe, step)
            logits(NG - 1, 1)

            def positions(r, par):
                pe.wait_ge(s["carry_done"], r + 1)
                wait(pe, s["slotv_done"], r)
                grp = chosen[:, bass.ds(r * GT, GT), :]
                ps = pos_ps
                mm(ps, earlier[:, :], grp, start=True, stop=False)
                mm(ps, mark[:, :], grp, start=False, stop=False)
                for q in range(GT - 1):
                    mm(ps[:, q + 1:GT, :], ones[:, :], chosen[:, bass.ds(r * GT + q, 1), :].to_broadcast([P, GT - 1 - q, E]),
                       start=False, stop=False)
                mm(ps, ones[:, :], carry[:, bass.ds(r, 1), :].to_broadcast([P, GT, E]), start=False, stop=True).then_inc(s["pos_done"], 1)

            def table_of(r, par):
                pe.wait_ge(s["onepos_done"], r + 1)
                pe.wait_ge(s["payload_done"], r + 1)
                for q in range(GT):
                    for k in range(TOPK):
                        last = mm(tab_ps, onepos[:, par, q, :, k], payload[:, par, q, :, k], start=False, stop=False)
                last.then_inc(s["tab_done"], 1)

            def unit(g, u):
                lo, m = SCH[u // 2]
                wait(pe, s["hT_done"], g * UNITS + u - 2)
                for w in range(2):
                    for k in range(KD):
                        last = mm(unit_ps[u % 3][0:m, w, :], sw13[:, k, w * SINTER + lo:w * SINTER + lo + m],
                                  yT_all[:, k, bass.ds(g * GTOK + (u % 2) * HTOK, HTOK)], start=(k == 0), stop=(k == KD - 1))
                last.then_inc(s["unit_done"], 1)

            def down(g):
                for h in range(2):
                    wait(pe, s["zadd_done"], g * 2 + h - 1)
                    pe.wait_ge(s["hT_done"], g * UNITS + (UNITS - 1) + h)
                    for q in range(2):
                        tok = (2 * h + q) * P
                        for c, (lo, m) in enumerate(SCH):
                            last = mm(z_ps[h][:, q, :], hT[0:m, c, tok:tok + P], sw2[0:m, c, :],
                                      start=(c == 0), stop=(c == len(SCH) - 1))
                    last.then_inc(s["z_done"], 1)

            pe.wait_ge(s["sw_in"], 48)
            pe.wait_ge(s["ycopy_done"], NG)

            def early(g):
                positions(g * 2, 0)
                for u in range(3):
                    unit(g, u)
                positions(g * 2 + 1, 1)
                for u in range(3, UNITS - 1):
                    unit(g, u)
                table_of(g * 2, 0)
                unit(g, UNITS - 1)
                down(g)
                table_of(g * 2 + 1, 1)

            pe.wait_ge(s["ytr_done"], NG * 2)
            pe.wait_ge(s["shift_done"], NG)
            early(0)
            with pe.Fori(1, EARLY - 1) as g:
                early(g)
            pe.wait_ge(s["slotv_done"], NG)
            mm(tab_ps, zeros_h[:, :], zeros_h[:, 0:E], start=False, stop=True)
            mm(cnt_ps, ones[:, :], carry[:, NG, :], start=True, stop=True).then_inc(s["tab_final"], 1)
            for u in range(UNITS):
                unit(EARLY - 1, u)
            down(EARLY - 1)

            def x_turn(e, slot):
                wait(pe, s["xeT_done"], e - 1)
                for k in range(KD):
                    last = nc.tensor.transpose(xeT_ps[slot % 2][:, k, :], xe[:, slot, k * P:(k + 1) * P], ident[:, :])
                last.then_inc(s["xt_done"], 1)

            def up(e, slot):
                pe.wait_ge(s["xeT_done"], e + 1)
                wait(pe, s["eh_done"], e - 1)
                for k in range(KD):
                    last = mm(h_ps[slot % 2], xeT[:, slot % 2, k, :], w13[:, slot, k, :], start=(k == 0), stop=(k == KD - 1))
                last.then_inc(s["h_done"], 1)

            def h_turn(e, slot):
                pe.wait_ge(s["eh_done"], e + 1)
                wait(pe, s["ehT_done"], e - 1)
                for k in range(2):
                    last = nc.tensor.transpose(ehT_ps[slot % 2][:, k, :], eh[:, slot % 2, k * IH:(k + 1) * IH], ident[:, :])
                last.then_inc(s["eht_done"], 1)

            def down_e(e, slot):
                pe.wait_ge(s["ehT_done"], e + 1)
                wait(pe, s["eyrow_done"], e - 1)
                for k in range(2):
                    last = mm(ey_ps[slot % 2], ehT[:, slot % 2, k, :], w2[:, slot, k, :], start=(k == 0), stop=(k == 1))
                last.then_inc(s["ey_done"], 1)

            def steady(e, slot, rounds, rounds_next):
                pe.wait_ge(xe_in[(slot + 1) % SLOTS], (rounds_next + 1) * 16)
                x_turn(e + 1, (slot + 1) % SLOTS)
                h_turn(e - 1, (slot - 1) % SLOTS)
                pe.wait_ge(w_in[slot], (rounds + 1) * 32)
                up(e, slot)
                down_e(e - 1, (slot - 1) % SLOTS)

            pe.wait_ge(s["hT_done"], EARLY * UNITS)
            pe.wait_ge(s["zadd_done"], EARLY * 2)
            pe.wait_ge(s["idx_done"], 1)
            for e in range(2):
                pe.wait_ge(xe_in[e], 16)
                x_turn(e, e)
            pe.wait_ge(w_in[0], 32)
            up(0, 0)
            for e in range(1, 1 + SLOTS):
                steady(e, e % SLOTS, e // SLOTS, (e + 1) // SLOTS)
            with pe.Fori(1, (E - SLOTS) // SLOTS) as it:
                for j in range(SLOTS):
                    e = 1 + j
                    steady(it * SLOTS + e, e % SLOTS, it + e // SLOTS, it + (e + 1) // SLOTS)
            for e in range(E - SLOTS + 1, E - 1):
                steady(e, e % SLOTS, e // SLOTS, (e + 1) // SLOTS)
            e = E - 1
            h_turn(e - 1, (e - 1) % SLOTS)
            pe.wait_ge(w_in[e % SLOTS], E // SLOTS * 32)
            up(e, e % SLOTS)
            down_e(e - 1, (e - 1) % SLOTS)
            h_turn(e, e % SLOTS)
            down_e(e, e % SLOTS)

            pe.wait_ge(s["eh_done"], E)
            pe.wait_ge(s["ehT_done"], E)
            for g in LATE:
                for u in range(UNITS):
                    unit(g, u)
                down(g)


def kernel(x, itok_B_0_7, fside_8xS_0, L0_cond_weights, L0_ffn_gate_w, L0_ffn_w1, L0_ffn_w2, L0_ffn_w3,
           L0_ffn_sw1, L0_ffn_sw2, L0_ffn_sw3):
    import concourse.bacc as bacc
    from concourse.bass_utils import run_bass_kernel_spmd

    w1, w3, w2 = np.asarray(L0_ffn_w1), np.asarray(L0_ffn_w3), np.asarray(L0_ffn_w2)
    up = np.concatenate([w1, w3], axis=1)
    lay = {
        "x": np.asarray(x),
        "subj": np.asarray(itok_B_0_7).reshape(B, 1),
        "table": np.concatenate([np.asarray(L0_cond_weights), np.asarray(fside_8xS_0)[:, :, None]], axis=2).reshape(NSUB, C * CW),
        "gate_t": np.asarray(L0_ffn_gate_w).T.reshape(KD, P, E).transpose(1, 0, 2),
        "w13_t": up.transpose(0, 2, 1).reshape(E, KD, P, 2 * INTER).transpose(0, 2, 1, 3),
        "w2_t": w2.transpose(0, 2, 1).reshape(E, 2, IH, D).transpose(0, 2, 1, 3),
        "sw13_t": np.concatenate([np.asarray(L0_ffn_sw1), np.asarray(L0_ffn_sw3)], axis=0).T.reshape(KD, P, 2 * SINTER).transpose(1, 0, 2),
        "sw2_t": np.asarray(L0_ffn_sw2).T,
    }
    nc = bacc.Bacc("TRN2", target_bir_lowering=False, num_devices=1)
    arrays, aps = {}, {}
    for name, a in lay.items():
        a = np.ascontiguousarray(a)
        arrays[name] = a
        aps[name] = nc.dram_tensor(name, a.shape, mybir.dt.from_np(a.dtype), kind="ExternalInput").ap()
    aps["out"] = nc.dram_tensor("out", (B, C, T), F32, kind="ExternalOutput").ap()
    build_adaln_moe(nc, **aps)
    r = run_bass_kernel_spmd(nc, [arrays], core_ids=[0])
    return r.results[0]["out"]
```

```python
import numpy as np
import concourse.bass as bass
from concourse import mybir
from contextlib import ExitStack

F32, I32, BF16, F16 = mybir.dt.float32, mybir.dt.int32, mybir.dt.bfloat16, mybir.dt.float16
F32R = mybir.dt.float32r
ACT, ALU, AX = mybir.ActivationFunctionType, mybir.AluOpType, mybir.AxisListType

B, C, T = 128, 32, 256
NSUB = 8
D = T
E, TOPK, INTER, CAP = 64, 6, 176, 128
SINTER = 2 * INTER
P = 128
N = B * C
NT = N // P
SPT = P // C
KD = D // P
GT = 4
NG = NT // GT
GTOK = GT * P
ROW = D + E
IH = INTER // 2
SCH = [(0, 128), (128, 128), (256, SINTER - 256)]
UNITS = 2 * len(SCH)
HTOK = GTOK // 2
EARLY = 5
NB = NG // 2
YSLOTS = 6
SPG = GTOK // C
SLOTS = 4
BUFS = 3
CW = C + 1
BIG = 3.0e38
GONE = -3.0e38
FLOOR = -87.3
UNCHOSEN = 64 * 128
HALF_N = N // 2


def wait(eng, sem, count):
    if not (isinstance(count, int) and count <= 0):
        eng.wait_ge(sem, count)


def wait_apart(eng, sem, count, passed):
    if not (isinstance(count, int) and count <= 0):
        eng.wait_ge(sem, count)
        eng.sem_inc(passed, 1)


def SLOT_OF(b, par):
    return (2 * b + par) % YSLOTS if isinstance(b, int) else b * -4 + (12 + par)


def build_adaln_moe(nc, x, subj, table, gate_t, w13_t, w2_t, sw13_t, sw2_t, out):
    x_rows = x.rearrange("b c t -> (b c) t").rearrange("(i p) t -> p i t", p=P)
    out_rows = out.rearrange("b c t -> (b c) t").rearrange("(i p) t -> p i t", p=P)

    ctx = ExitStack()
    with ctx:
        def sb(name, shape, dt):
            return ctx.enter_context(nc.sbuf_tensor(name, shape, dt))

        def sem(name):
            return ctx.enter_context(nc.semaphore(name))

        rows_dram = nc.dram_tensor("rows_dram", (N, ROW), F32).ap()
        acc_dram = [nc.dram_tensor(f"acc{a}_dram", (N + CAP, D), F32).ap() for a in range(2)]
        rows_tiles = rows_dram.rearrange("(i p) n -> p i n", p=P)
        acc_tiles = [a[0:N, :].rearrange("(i p) n -> p i n", p=P) for a in acc_dram]

        x_all = sb("x_all", [P, NT, D], F32)
        yhi = sb("yhi", [P, KD, YSLOTS * GTOK], F32R)
        ylo = sb("ylo", [P, KD, YSLOTS * GTOK], F32R)
        sw13hi = sb("sw13hi", [P, KD, 2 * SINTER], F32R)
        sw13lo = sb("sw13lo", [P, KD, 2 * SINTER], F32R)
        sw2hi = sb("sw2hi", [P, len(SCH), D], F32R)
        sw2lo = sb("sw2lo", [P, len(SCH), D], F32R)
        gate_sb = sb("gate_sb", [P, KD, E], F32)
        subj_sb = sb("subj_sb", [P, B], I32)
        subj32 = sb("subj32", [P, B + 2 * SPG, 2], BF16)
        table_sb = sb("table_sb", [P, 2, CW], F32)
        tab3 = sb("tab3", [P, 2, 3, CW], BF16)
        tab_left = sb("tab_left", [P, 2, 2, CW], F32)
        rowdiff = sb("rowdiff", [P, 2, C], BF16)
        bias = sb("bias", [P, 2, GT], F32)
        wblk = sb("wblk", [P, 2, GT, P], F32)
        blocks = sb("blocks", [P, SPT, C], F32)
        ytr = sb("ytr", [P, GT, KD, P], F32)
        front = sb("front", [P, max(2 * GT * D + 2 * GTOK, SLOTS * (ROW + D) + 4 * D + 4 * INTER)], F32)
        yrow = front[:, 0:2 * GT * D].rearrange("p (a q n) -> p a q n", a=2, q=GT)
        sel = front[:, 2 * GT * D:2 * GT * D + 2 * GTOK].bitcast(BF16).rearrange("p (a h n) -> p a h n", a=2, h=2)

        def carve(start, *shape):
            size = int(np.prod(shape))
            names = "abc"[:len(shape)]
            v = front[:, start:start + size].rearrange(
                f"p ({' '.join(names)}) -> p {' '.join(names)}", **dict(zip(names, shape)))
            return v, start + size

        xe, at = carve(0, SLOTS, ROW)
        ey, at = carve(at, SLOTS, D)
        xeT, at = carve(at, 2, KD, P)
        ehT, at = carve(at, 2, 2, P)
        eg, at = carve(at, 2, INTER)
        eh, at = carve(at, 2, INTER)
        key = sb("key", [P, 2, GT, E + 2], F32)
        left = sb("left", [P, GT, E + 2], F32)
        rowmax = sb("rowmax", [P, GT], F32)
        top8 = sb("top8", [P, GT, 8], F32)
        chosen = sb("chosen", [P, NT, E], BF16)
        pair = sb("pair", [P, 2, E], F32)
        gsum = sb("gsum", [P, E], F32)
        carry = sb("carry", [P, NG + 1, E], BF16)
        exps = sb("exps", [P, 2, GT, E], F32)
        esum = sb("esum", [P, 2, GT], F32)
        rsum = sb("rsum", [P, 2, GT], F32)
        scores = sb("scores", [P, 2, GT, E], F32)
        slot1 = sb("slot1", [P, GT, E], F32)
        slotv = sb("slotv", [P, GT, E], F32)
        s8 = sb("s8", [P, GT, 8], F32)
        slot_i = sb("slot_i", [P, GT, 8], I32)
        pos_i = sb("pos_i", [P, GT, 8], I32)
        exp_i = sb("exp_i", [P, GT, 8], I32)
        pos_h = sb("pos_h", [P, GT, 8], F16)
        exp_h = sb("exp_h", [P, GT, 8], F16)
        back = sb("back", [P, 2 * GT * (P + 2 * E) * TOPK], F16)
        n_pos, n_exp = 2 * GT * P * TOPK, 2 * GT * E * TOPK
        onepos = back[:, 0:n_pos].rearrange("p (a q c k) -> p a q c k", a=2, q=GT, k=TOPK)
        oneexp = back[:, n_pos:n_pos + n_exp].rearrange("p (a q c k) -> p a q c k", a=2, q=GT, k=TOPK)
        payload = back[:, n_pos + n_exp:].rearrange("p (a q c k) -> p a q c k", a=2, q=GT, k=TOPK)
        n_sw13, n_sw2 = 2 * KD * 2 * SINTER, 2 * len(SCH) * D
        sw13 = back[:, 0:n_sw13].bitcast(F32).rearrange("p (k n) -> p k n", k=KD)
        sw2 = back[:, n_sw13:n_sw13 + n_sw2].bitcast(F32).rearrange("p (m n) -> p m n", m=len(SCH))
        acc_sb = [back[:, a * 2 * BUFS * GT * D:(a + 1) * 2 * BUFS * GT * D].bitcast(F32).rearrange("p (i q n) -> p i q n", i=BUFS, q=GT)
                  for a in range(2)]
        idxf = sb("idxf", [P, E], F32)
        empty = sb("empty", [P, E], F32)
        idx_read = sb("idx_read", [P, E], I32)
        idx_write = sb("idx_write", [P, E], I32)
        sg = sb("sg", [P, 2, HTOK], F32)
        hf = sb("hf", [P, 2, HTOK], F32)
        hThi = sb("hThi", [P, len(SCH), GTOK], F32R)
        hTlo = sb("hTlo", [P, len(SCH), GTOK], F32R)
        w13 = sb("w13", [P, SLOTS, KD, 2 * INTER], F32)
        w2 = sb("w2", [IH, SLOTS, 2, D], F32)
        ri = sb("ri", [P, SLOTS, 1], I32)
        wi = sb("wi", [P, SLOTS, 1], I32)
        ident = sb("ident", [P, P], F32)
        earlier = sb("earlier", [P, P], BF16)
        mark = sb("mark", [P, P], BF16)
        ones = sb("ones", [P, P], BF16)
        zeros_h = sb("zeros_h", [P, P], F16)
        zeros = sb("zeros", [P, 1024], F32)
        iota_p = sb("iota_p", [P, 1], F32)
        warm = sb("warm", [P, 1], F32)
        ids_i = sb("ids_i", [P, NT], I32)
        ids = sb("ids", [P, NT], F32)
        dump_p = sb("dump_p", [P, 1], F32)
        slot0 = sb("slot0", [P, E], F32)
        iota_c = sb("iota_c", [P, P, TOPK], F16)
        iota_e = iota_c[:, 0:E, :]

        bank = [ctx.enter_context(nc.psum_tensor(f"bank{i}", [P, 512], F32)) for i in range(8)]

        unit_ps = [bank[i][:, :].rearrange("p (w t) -> p w t", w=2) for i in range(2)]
        selw_ps = [bank[2 + a][:, 0:GT * CW].rearrange("p (q w) -> p q w", q=GT) for a in range(2)]
        yT_ps = [bank[2 + h][:, :].rearrange("p (q k c) -> p q k c", q=2, k=KD) for h in range(2)]
        y_ps = [bank[4 + h][:, :].rearrange("p (q n) -> p q n", q=2) for h in range(2)]
        z_ps = y_ps
        lg_ps = bank[6][:, 0:GT * E].rearrange("p (q e) -> p q e", q=GT)
        pos_ps = lg_ps
        cnt_ps = bank[6][:, 0:E]
        tab_ps = bank[7][:, 0:E]
        xeT_ps = [bank[0 + i][:, 0:D].rearrange("p (k c) -> p k c", k=KD) for i in range(2)]
        h_ps = [bank[2 + i][:, 0:2 * INTER] for i in range(2)]
        ehT_ps = [bank[4 + i][0:IH, 0:2 * P].rearrange("p (k c) -> p k c", k=2) for i in range(2)]
        ey_ps = [bank[6 + i][:, 0:D] for i in range(2)]

        s = {}
        for name in (
            "pool_const", "dve_passed", "pool_passed", "block_zero", "block_one", "dve_const", "consts", "subj_in", "table_in",
            "gate_in", "sw_in", "subj32_done", "tab3_done", "tab_left_done", "sel_done", "selw_done", "bias_done", "wblk_done", "swhi_done", "swlo_done",
            "yhi_done", "ylo_done", "hf_done", "hThi_done", "sum_done", "y_done", "yrow_done", "yT_done", "ytr_done", "lg_done",
            "rowmax_done", "shift_done", "key_done", "top8_done", "left_done", "chosen_done", "pair_done", "gsum_done",
            "carry_done", "exp_done", "esum_done", "warm_done", "recip_done", "score_done", "p_stored",
            "pos_done", "slot1_done", "slotv_done", "s8_done", "sloti_done", "split_done", "code_done",
            "onepos_done", "oneexp_done", "payload_done", "tab_done", "tab_final", "idxf_done", "empty_done", "idx_done",
            "unit_done", "silu_done", "z_done", "zadd_done",
            "acc_zero", "ri_done", "wi_done", "xt_done", "xeT_done", "h_done", "eg_done", "eh_done",
            "eht_done", "ehT_done", "ey_done", "eyrow_done",
            "hTlo_done", "combined", "out_stored",
        ):
            s[name] = sem(name)
        x_in = [sem(f"x_in{i}") for i in range(2)]
        y_stored = [sem(f"y_stored{i}") for i in range(2)]
        w_in = [sem(f"w_in{i}") for i in range(SLOTS)]
        xe_in = [sem(f"xe_in{i}") for i in range(SLOTS)]
        acc_added = [sem(f"acc_added{i}") for i in range(2)]
        acc_in = [sem(f"acc_in{i}") for i in range(BUFS)]

        block = ctx.enter_context(nc.Block())

        def over_bodies(eng, body):
            body(0)
            body(1)
            with eng.Fori(2, NB) as b:
                body(b)

        def landed(e, slot):
            if isinstance(e, int):
                return ((e - SLOTS) // 2 + 1) * 16 if e >= SLOTS else 0
            return e * 8 - (SLOTS + slot % 2) * 8 + 16

        LATE = list(range(EARLY, NG))
        PAYS = {(NB - 1, 4): NG - 3, (NB, 0): NG - 2, (NB, 2): NG - 1}
        ORDER = [0, 1, 5, 2, 6, 7, 3, 4]
        AFTER = [(5, 5), (6, 1), (6, 3), (6, 5), (7, 1), (7, 4), (7, 5), None]

        @block.sync
        def _(sp):
            sp.dma_start(subj_sb[:, :], subj.to_broadcast([P, B])).then_inc(s["subj_in"], 16)
            sp.dma_start(table_sb[:, :, :], table.rearrange("(h p) w -> p h w", p=P)).then_inc(s["table_in"], 16)
            per = zeros.shape[1] // D
            acc_flat = [acc_dram[a][0:N, :].rearrange("(r p n) d -> r p (n d)", p=P, n=per) for a in range(2)]

            def load_group(g):
                sp.dma_start(x_all[:, g * GT:(g + 1) * GT, :], x_rows[:, g * GT:(g + 1) * GT, :]).then_inc(x_in[g % 2], 16)

            def store_scores(b):
                sp.wait_ge(s["score_done"], b + 1)
                sp.dma_start(rows_tiles[:, 2 * b * GT:2 * (b + 1) * GT, D:ROW],
                             scores.rearrange("p a q e -> p (a q) e")).then_inc(s["p_stored"], 16)

            def start_sum(g):
                sp.wait_ge(s["zadd_done"], g * 2 + 2)
                sp.dma_start(acc_tiles[0][:, g * GT:(g + 1) * GT, :], x_all[:, g * GT:(g + 1) * GT, :]).then_inc(s["acc_zero"], 16)

            load_group(0)
            load_group(1)
            sp.dma_start(gate_sb[:, :, :], gate_t).then_inc(s["gate_in"], 16)
            sp.dma_start(sw13[:, :, :], sw13_t).then_inc(s["sw_in"], 16)
            sp.dma_start(sw2[:, 0:2, :], sw2_t[0:2 * P, :].rearrange("(m p) n -> p m n", p=P)).then_inc(s["sw_in"], 16)
            sp.dma_start(sw2[0:SCH[2][1], 2, :], sw2_t[2 * P:SINTER, :]).then_inc(s["sw_in"], 16)
            sp.wait_ge(s["consts"], 1)
            for a in range(2):
                sp.dma_start(acc_dram[a][N:N + CAP, :], zeros[:, 0:D]).then_inc(s["acc_zero"], 16)
            for g in range(NG):
                if g + 2 < NG:
                    sp.wait_ge(x_in[g % 2], (g // 2 + 1) * 16)
                    load_group(g + 2)
                for a in range(2):
                    if a == 1 or g in LATE:
                        sp.dma_start(acc_flat[a][g], zeros[:, :]).then_inc(s["acc_zero"], 16)
                sp.wait_ge(s["yrow_done"], g * GT + GT)
                sp.dma_start(rows_tiles[:, g * GT:(g + 1) * GT, 0:D], yrow[:, g % 2, :, :]).then_inc(y_stored[g % 2], 16)
                if g % 2 == 1 and g > 1:
                    store_scores(g // 2 - 1)
                    if g > 3:
                        start_sum(g // 2 - 2)
            store_scores(NB - 1)

            def load_expert(e, slot):
                wait(sp, s["ey_done"], e - SLOTS + 1)
                sp.dma_start(w13[:, slot, :, :], w13_t[bass.ds(e, 1)].rearrange("a p k n -> p (a k) n")).then_inc(w_in[slot], 16)
                sp.dma_start(w2[:, slot, :, :], w2_t[bass.ds(e, 1)].rearrange("a p k n -> p (a k) n")).then_inc(w_in[slot], 16)

            for slot in range(SLOTS):
                load_expert(slot, slot)
            for g in range(NB - 2, EARLY):
                start_sum(g)
            with sp.Fori(1, E // SLOTS) as it:
                for slot in range(SLOTS):
                    load_expert(it * SLOTS + slot, slot)

            for a in range(2):
                sp.wait_ge(acc_added[a], E // 2 * 16)

            def load_sums(n):
                g = ORDER[n]
                for a in range(2):
                    sp.dma_start(acc_sb[a][:, n % BUFS, :, :], acc_tiles[a][:, g * GT:(g + 1) * GT, :]).then_inc(acc_in[n % BUFS], 16)

            def store_result(g, tiles):
                i = g * GT + tiles[0]
                sp.dma_start(out_rows[:, i:i + len(tiles), :], x_all[:, i:i + len(tiles), :]).then_inc(s["out_stored"], 16)

            for n in range(BUFS):
                load_sums(n)
            for n in range(NG):
                sp.wait_ge(s["combined"], n + 1)
                if n + BUFS < NG:
                    load_sums(n + BUFS)
                if ORDER[n] < EARLY:
                    store_result(ORDER[n], range(GT))
                if n == NG - 4:
                    sp.wait_ge(s["zadd_done"], (LATE[0] + 1) * 2)
                    store_result(LATE[0], range(GT))
                if n == NG - 3:
                    sp.wait_ge(s["zadd_done"], (LATE[1] + 1) * 2)
                    store_result(LATE[1], range(GT))
            for h in range(2):
                sp.wait_ge(s["zadd_done"], (NG - 1) * 2 + h + 1)
                store_result(NG - 1, range(2 * h, 2 * h + 2))
            sp.wait_ge(s["out_stored"], (NG + 1) * 16)

        @block.gpsimd
        def _(pool):
            nc.gpsimd.memset(ident[:, :], 1.0)
            nc.gpsimd.memset(earlier[:, :], 1.0)
            nc.gpsimd.memset(mark[:, :], -float(UNCHOSEN))
            nc.gpsimd.memset(ones[:, :], 1.0)
            nc.gpsimd.memset(zeros_h[:, :], 0.0)
            nc.gpsimd.memset(zeros[:, :], 0.0)
            nc.gpsimd.iota(rowdiff[:, :, :], [[P, 2], [-1, C]], base=0, channel_multiplier=1, allow_small_or_imprecise_dtypes=True)
            nc.gpsimd.memset(carry[:, 0, :], 0.0)
            nc.gpsimd.memset(key[:, :, :, E:E + 2], BIG).then_inc(s["pool_const"], 1)
            pool.wait_ge(s["pool_const"], 1)
            nc.gpsimd.affine_select(out=ident[:, :], in_=ident[:, :], compare_op=ALU.is_equal, fill=0.0,
                                    base=0, pattern=[[-1, P]], channel_multiplier=1)
            nc.gpsimd.affine_select(out=mark[:, :], in_=mark[:, :], compare_op=ALU.is_equal, fill=0.0,
                                    base=0, pattern=[[-1, P]], channel_multiplier=1)
            nc.gpsimd.affine_select(out=earlier[:, :], in_=earlier[:, :], compare_op=ALU.is_gt, fill=0.0,
                                    base=0, pattern=[[1, P]], channel_multiplier=-1)
            nc.gpsimd.iota(iota_p[:, :], [[1, 1]], base=0, channel_multiplier=1, allow_small_or_imprecise_dtypes=True)
            nc.gpsimd.iota(dump_p[:, :], [[1, 1]], base=HALF_N, channel_multiplier=1, allow_small_or_imprecise_dtypes=True)
            nc.gpsimd.iota(ids_i[:, :], [[P, NT]], base=-HALF_N, channel_multiplier=1)
            nc.gpsimd.iota(slot0[:, :], [[CAP, E]], base=UNCHOSEN + 1, channel_multiplier=0,
                           allow_small_or_imprecise_dtypes=True)
            nc.gpsimd.iota(iota_c[:, :, :], [[1, P], [0, TOPK]], base=0, channel_multiplier=0,
                           allow_small_or_imprecise_dtypes=True).then_inc(s["consts"], 1)

            def left_of_h(g, u):
                m = SCH[u // 2][1]
                where = (slice(0, m), u // 2, slice((u % 2) * HTOK, (u % 2 + 1) * HTOK))
                pool.wait_ge(s["hThi_done"], g * UNITS + u + 1)
                nc.gpsimd.tensor_tensor(hTlo[where], hf[0:m, u % 2, :], hThi[where].bitcast(F32),
                                        ALU.subtract).then_inc(s["hTlo_done"], 1)

            def carry_of(g):
                pool.wait_ge(s["chosen_done"], g + 1)
                wait(pool, s["carry_done"], g)
                nc.gpsimd.tensor_tensor(pair[:, :, :], chosen[:, g * GT:g * GT + 2, :], chosen[:, g * GT + 2:g * GT + 4, :],
                                        ALU.add).then_inc(s["pair_done"], 1)
                pool.wait_ge(s["pair_done"], g + 1)
                nc.gpsimd.tensor_tensor(gsum[:, :], pair[:, 0, :], pair[:, 1, :], ALU.add).then_inc(s["gsum_done"], 1)
                pool.wait_ge(s["gsum_done"], g + 1)
                nc.gpsimd.tensor_tensor(carry[:, g + 1, :], carry[:, g, :],
                                        gsum[:, :], ALU.add).then_inc(s["carry_done"], 1)

            def scores_of(b):
                pool.wait_ge(s["recip_done"], b + 1)
                wait(pool, s["p_stored"], b * 16)
                nc.gpsimd.tensor_tensor(scores[:, :, :, :], exps[:, :, :, :],
                                        rsum[:, :, :].unsqueeze(3).to_broadcast([P, 2, GT, E]),
                                        ALU.mult).then_inc(s["score_done"], 1)

            def left_of_y(g, slot):
                pool.wait_ge(s["yhi_done"], g + 1)
                for k in range(KD):
                    where = (slice(None), k, slice(slot * GTOK, (slot + 1) * GTOK))
                    last = nc.gpsimd.tensor_tensor(ylo[where].rearrange("p (q c) -> p q c", q=GT), ytr[:, :, k, :],
                                                   yhi[where].bitcast(F32).rearrange("p (q c) -> p q c", q=GT), ALU.subtract)
                last.then_inc(s["ylo_done"], 1)

            for b in range(NB + 1):
                shared, cond = b > 0, b < NB
                if shared:
                    carry_of(b * 2 - 1)
                    left_of_h(b - 1, 0)
                    left_of_h(b - 1, 1)
                if shared and cond:
                    scores_of(b - 1)
                if shared:
                    left_of_h(b - 1, 2)
                if cond:
                    left_of_y(b * 2, (b * 2) % YSLOTS)
                if shared:
                    left_of_h(b - 1, 3)
                    left_of_h(b - 1, 4)
                    left_of_h(b - 1, 5)
                if cond:
                    carry_of(b * 2)
                    left_of_y(b * 2 + 1, (b * 2 + 1) % YSLOTS)

            scores_of(NB - 1)
            for u in range(UNITS):
                left_of_h(NB, u)

            for par in range(2):
                pool.wait_ge(y_stored[par], NG // 2 * 16)
            pool.wait_ge(s["p_stored"], NB * 16)
            pool.wait_ge(s["idx_done"], 1)

            def gather(e, slot, rounds):
                if rounds is not None:
                    pool.wait_ge(s["xt_done"], e - SLOTS + 1)
                    pool.wait_ge(s["eh_done"], e - SLOTS + 1)
                wait_apart(pool, s["ri_done"], e + 1, s["pool_passed"])
                pool.indirect_dma_start(xe[:, slot, :], None, rows_dram, bass.IndirectOffsetOnAxis(ri[:, slot, 0:1], 0),
                                        bounds_check=N - 1, oob_is_err=False).then_inc(xe_in[slot], 16)

            def scatter(e, slot):
                a = slot % 2
                wait(pool, acc_added[a], (e - slot) // 2 * 16 + slot // 2 * 16 if isinstance(e, int) else e * 8 - a * 8)
                wait_apart(pool, s["wi_done"], e + 1, s["pool_passed"])
                wait_apart(pool, s["eyrow_done"], e + 1, s["pool_passed"])
                pool.indirect_dma_start(acc_dram[a], bass.IndirectOffsetOnAxis(wi[:, slot, 0:1], 0), ey[:, slot, :], None,
                                        bounds_check=N + CAP - 1, oob_is_err=True, compute_op=ALU.add).then_inc(acc_added[a], 16)

            for slot in range(SLOTS):
                gather(slot, slot, None)
            pool.wait_ge(s["acc_zero"], 2 * (NG + 1) * 16)
            for slot in range(SLOTS):
                gather(SLOTS + slot, slot, 1)
                scatter(slot, slot)
            with pool.Fori(1, E // SLOTS - 1) as it:
                for slot in range(SLOTS):
                    gather(it * SLOTS + (SLOTS + slot), slot, it + 1)
                    scatter(it * SLOTS + slot, slot)
            for slot in range(SLOTS):
                scatter(E - SLOTS + slot, slot)

            for n in range(NG):
                if ORDER[n] in LATE:
                    both = acc_sb[0][:, n % BUFS, :, :]
                    pool.wait_ge(acc_in[n % BUFS], (n // BUFS + 1) * 32)
                    nc.gpsimd.tensor_tensor(both, both, acc_sb[1][:, n % BUFS, :, :], ALU.add).then_inc(s["sum_done"], 1)

        @block.scalar
        def _(act):
            act.wait_ge(s["sw_in"], 48)
            nc.scalar.copy(sw13hi[:, :, :], sw13[:, :, :])
            nc.scalar.copy(sw2hi[:, 0:2, :], sw2[:, 0:2, :])
            nc.scalar.copy(sw2hi[0:SCH[2][1], 2, :], sw2[0:SCH[2][1], 2, :]).then_inc(s["swhi_done"], 1)

            def take_rows(g, par, rounds):
                act.wait_ge(s["bias_done"], g + 1)
                wait(act, y_stored[par], rounds * 16)
                for q in range(GT):
                    act.wait_ge(s["y_done"], g * 2 + q // 2 + 1)
                    nc.scalar.activation(yrow[:, par, q, :], y_ps[q // 2][:, q % 2, :], ACT.Identity,
                                         bias=bias[:, par, q:q + 1]).then_inc(s["yrow_done"], 1)

            def take_yT(g):
                wait(act, s["lg_done"], g)
                wait(act, s["ylo_done"], g)
                for h in range(2):
                    act.wait_ge(s["yT_done"], g * 2 + h + 1)
                    nc.scalar.copy(ytr[:, 2 * h:2 * h + 2, :, :], yT_ps[h]).then_inc(s["ytr_done"], 1)

            def round_y(g, slot, b):
                act.wait_ge(s["ytr_done"], g * 2 + 2)
                wait(act, s["unit_done"], b * UNITS - UNITS)
                for k in range(KD):
                    last = nc.scalar.copy(yhi[:, k, bass.ds(slot * GTOK, GTOK)].rearrange("p (q c) -> p q c", q=GT), ytr[:, :, k, :])
                last.then_inc(s["yhi_done"], 1)

            def load_table(function, before):
                wait(act, s["warm_done"], before)
                nc.scalar.activation(warm[:, :], zeros[:, 0:1], function).then_inc(s["warm_done"], 1)

            def exp_of(b):
                act.wait_ge(s["consts"], 1)
                load_table(ACT.Exp, b * 2)
                act.wait_ge(s["key_done"], b * 2 + 2)
                wait(act, s["score_done"], b)
                nc.scalar.activation(exps[:, :, :, :], key[:, :, :, 0:E], ACT.Exp).then_inc(s["exp_done"], 1)
                load_table(ACT.Silu, b * 2 + 1)

            def silu(g, u):
                m = SCH[u // 2][1]
                act.wait_ge(s["unit_done"], g * UNITS + u + 1)
                wait(act, s["hf_done"], g * UNITS + u - 1)
                nc.scalar.activation(sg[0:m, u % 2, :], unit_ps[u % 2][0:m, 0, :], ACT.Silu).then_inc(s["silu_done"], 1)

            def round_h(g, u):
                m = SCH[u // 2][1]
                act.wait_ge(s["hf_done"], g * UNITS + u + 1)
                wait(act, s["z_done"], g * 2)
                nc.scalar.copy(hThi[0:m, u // 2, (u % 2) * HTOK:(u % 2 + 1) * HTOK], hf[0:m, u % 2, :]).then_inc(s["hThi_done"], 1)

            def pay(r, par, tables=None):
                act.wait_ge(s["oneexp_done"], r + 1)
                wait(act, s["tab_done"], r - 1 if tables is None else tables)
                for q in range(GT):
                    last = nc.scalar.activation(payload[:, par, q, :, :], oneexp[:, par, q, :, :], ACT.Copy,
                                                scale=ids[:, bass.ds(r * GT + q, 1)])
                last.then_inc(s["payload_done"], 1)

            def body(b):
                shared = not (isinstance(b, int) and b == 0)
                behind = not (isinstance(b, int) and b <= 1)
                if shared:
                    silu(b - 1, 0)
                    round_h(b - 1, 0)
                take_rows(b * 2, 0, b)
                if shared:
                    silu(b - 1, 1)
                    round_h(b - 1, 1)
                take_yT(b * 2)
                round_y(b * 2, SLOT_OF(b, 0), b)
                if behind:
                    pay(b * 2 - 3, 1, b * 2 - 3)
                if shared:
                    silu(b - 1, 2)
                    round_h(b - 1, 2)
                    silu(b - 1, 3)
                take_rows(b * 2 + 1, 1, b)
                if shared:
                    round_h(b - 1, 3)
                    silu(b - 1, 4)
                take_yT(b * 2 + 1)
                if shared:
                    round_h(b - 1, 4)
                    silu(b - 1, 5)
                round_y(b * 2 + 1, SLOT_OF(b, 1), b)
                if shared:
                    round_h(b - 1, 5)
                    pay(b * 2 - 2, 0)
                exp_of(b)

            over_bodies(act, body)
            for g in (NB - 1, NB):
                for u in range(UNITS):
                    silu(g, u)
                    if (g, u) in PAYS:
                        r = PAYS[g, u]
                        pay(r, r % 2)
                    round_h(g, u)

            def take_xT(e, slot):
                act.wait_ge(s["xt_done"], e + 1)
                wait(act, s["h_done"], e - 1)
                nc.scalar.copy(xeT[:, slot % 2, :, :], xeT_ps[slot % 2]).then_inc(s["xeT_done"], 1)

            def take_h(e, slot):
                act.wait_ge(s["h_done"], e + 1)
                wait(act, s["eh_done"], e - 1)
                nc.scalar.activation(eg[:, slot % 2, :], h_ps[slot % 2][:, 0:INTER], ACT.Silu).then_inc(s["eg_done"], 1)

            def take_y(e, slot):
                act.wait_ge(s["ey_done"], e + 1)
                wait(act, acc_added[slot % 2], landed(e, slot))
                nc.scalar.copy(ey[:, slot, :], ey_ps[slot % 2]).then_inc(s["eyrow_done"], 1)

            def steady(e, slot):
                take_xT(e + 1, slot + 1)
                take_h(e, slot)
                take_y(e - 1, (slot - 1) % SLOTS)

            take_xT(0, 0)
            take_xT(1, 1)
            take_h(0, 0)
            for e in range(1, 1 + SLOTS):
                steady(e, e % SLOTS)
            with act.Fori(1, (E - SLOTS) // SLOTS) as it:
                for j in range(SLOTS):
                    steady(it * SLOTS + (1 + j), (1 + j) % SLOTS)
            for e in range(E - SLOTS + 1, E - 1):
                steady(e, e % SLOTS)
            take_h(E - 1, (E - 1) % SLOTS)
            take_y(E - 2, (E - 2) % SLOTS)
            take_y(E - 1, (E - 1) % SLOTS)

            for g in LATE:
                for u in range(UNITS):
                    silu(g, u)
                    round_h(g, u)

        @block.vector
        def _(dve):
            nc.vector.memset(blocks[:, :, :], 0.0).then_inc(s["block_zero"], 1)
            dve.wait_ge(s["block_zero"], 1)
            for j in range(SPT):
                last = nc.vector.memset(blocks[j * C:(j + 1) * C, j, :], 1.0)
            last.then_inc(s["block_one"], 1)
            dve.wait_ge(s["consts"], 1)
            dve.wait_ge(s["subj_in"], 16)
            nc.vector.memset(subj32[:, B:, :], 0.0)
            nc.vector.tensor_scalar(subj32[:, 0:B, :], subj_sb[:, :].unsqueeze(2).to_broadcast([P, B, 2]), float(C), None, ALU.mult).then_inc(s["subj32_done"], 1)
            dve.wait_ge(s["table_in"], 16)
            nc.vector.tensor_copy(tab3[:, :, 0, :], table_sb[:, :, :]).then_inc(s["tab3_done"], 1)
            dve.wait_ge(s["tab3_done"], 1)
            nc.vector.tensor_tensor(tab_left[:, 0, :, :], table_sb[:, :, :], tab3[:, :, 0, :], ALU.subtract).then_inc(s["tab_left_done"], 1)
            dve.wait_ge(s["tab_left_done"], 1)
            nc.vector.tensor_copy(tab3[:, :, 1, :], tab_left[:, 0, :, :]).then_inc(s["tab3_done"], 1)
            dve.wait_ge(s["tab3_done"], 2)
            nc.vector.tensor_tensor(tab_left[:, 1, :, :], tab_left[:, 0, :, :], tab3[:, :, 1, :], ALU.subtract).then_inc(s["tab_left_done"], 1)
            dve.wait_ge(s["tab_left_done"], 2)
            nc.vector.tensor_copy(tab3[:, :, 2, :], tab_left[:, 1, :, :]).then_inc(s["tab3_done"], 1)
            nc.vector.tensor_copy(ids[:, :], ids_i[:, :]).then_inc(s["dve_const"], 1)

            def build_blocks(g, par):
                dve.wait_ge(s["selw_done"], g + 1)
                wait(dve, s["yrow_done"], (g - 1) * GT)
                nc.vector.tensor_copy(bias[:, par, :], selw_ps[par][:, :, C]).then_inc(s["bias_done"], 1)
                nc.vector.tensor_tensor(wblk[:, par, :, :].rearrange("p q (j d) -> p q j d", j=SPT),
                                        selw_ps[par][:, :, 0:C].unsqueeze(2).to_broadcast([P, GT, SPT, C]),
                                        blocks[:, :, :].unsqueeze(1).to_broadcast([P, GT, SPT, C]),
                                        ALU.mult).then_inc(s["wblk_done"], 1)

            def select(b):
                wait(dve, s["selw_done"], b * 2)
                for par in range(2):
                    for h in range(2):
                        last = nc.vector.tensor_tensor(
                            sel[:, par, h, :].rearrange("p (s c e) -> p s c e", c=C // 2, e=2),
                            subj32[:, bass.ds(b * (2 * SPG) + par * SPG, SPG), :].unsqueeze(2).to_broadcast([P, SPG, C // 2, 2]),
                            rowdiff[:, h, :].rearrange("p (c e) -> p c e", e=2).unsqueeze(1).to_broadcast([P, SPG, C // 2, 2]),
                            ALU.is_equal)
                    last.then_inc(s["sel_done"], 1)

            def shifted_logits(g, par, b):
                lg = lg_ps
                dve.wait_ge(s["lg_done"], g + 1)
                nc.vector.tensor_reduce(rowmax[:, :], lg, AX.X, ALU.max).then_inc(s["rowmax_done"], 1)
                dve.wait_ge(s["rowmax_done"], g + 1)
                wait(dve, s["exp_done"], b)
                k64 = key[:, par, :, 0:E]
                nc.vector.tensor_tensor(k64, lg, rowmax[:, :].unsqueeze(2).to_broadcast([P, GT, E]),
                                        ALU.subtract).then_inc(s["shift_done"], 1)
                dve.wait_ge(s["shift_done"], g + 1)
                nc.vector.tensor_scalar(k64, k64, FLOOR, None, ALU.max).then_inc(s["key_done"], 1)

            def choose(g, par):
                wait_apart(dve, s["key_done"], g + 1, s["dve_passed"])
                for q in range(GT):
                    last = nc.vector.max(top8[:, q, :], key[:, par, q, :])
                last.then_inc(s["top8_done"], 1)
                wait_apart(dve, s["top8_done"], g + 1, s["dve_passed"])
                for q in range(GT):
                    last = nc.vector.match_replace(left[:, q, :], top8[:, q, :], key[:, par, q, :], GONE)
                last.then_inc(s["left_done"], 1)
                dve.wait_ge(s["left_done"], g + 1)
                mine = chosen[:, bass.ds(g * GT, GT), :]
                nc.vector.tensor_tensor(mine, left[:, :, 0:E], key[:, par, :, 0:E], ALU.is_lt).then_inc(s["chosen_done"], 1)

            def sums_of(b):
                dve.wait_ge(s["exp_done"], b + 1)
                nc.vector.tensor_reduce(esum[:, :, :], exps[:, :, :, :], AX.X, ALU.add).then_inc(s["esum_done"], 1)
                dve.wait_ge(s["esum_done"], b + 1)
                wait(dve, s["score_done"], b)
                nc.vector.reciprocal(rsum[:, :, :], esum[:, :, :]).then_inc(s["recip_done"], 1)

            def slots_of(r):
                dve.wait_ge(s["pos_done"], r + 1)
                nc.vector.tensor_tensor(slot1[:, :, :], pos_ps, slot0[:, :].unsqueeze(1).to_broadcast([P, GT, E]),
                                        ALU.add).then_inc(s["slot1_done"], 1)
                dve.wait_ge(s["slot1_done"], r + 1)
                nc.vector.scalar_tensor_tensor(slotv[:, :, :], pos_ps, float(CAP - UNCHOSEN), slot1[:, :, :],
                                               ALU.is_lt, ALU.mult).then_inc(s["slotv_done"], 1)

            def codes_of(r):
                wait_apart(dve, s["slotv_done"], r + 1, s["dve_passed"])
                for q in range(GT):
                    last = nc.vector.max(s8[:, q, :], slotv[:, q, :])
                last.then_inc(s["s8_done"], 1)
                dve.wait_ge(s["s8_done"], r + 1)
                nc.vector.tensor_scalar(slot_i[:, :, :], s8[:, :, :], -1.0, None, ALU.add).then_inc(s["sloti_done"], 1)
                dve.wait_ge(s["sloti_done"], r + 1)
                nc.vector.tensor_scalar(pos_i[:, :, :], slot_i[:, :, :], CAP - 1, None, ALU.bitwise_and)
                nc.vector.tensor_scalar(exp_i[:, :, :], slot_i[:, :, :], 7, None, ALU.arith_shift_right).then_inc(s["split_done"], 1)
                dve.wait_ge(s["split_done"], r + 1)
                nc.vector.tensor_copy(pos_h[:, :, :], pos_i[:, :, :])
                nc.vector.tensor_copy(exp_h[:, :, :], exp_i[:, :, :]).then_inc(s["code_done"], 1)

            def one_hot_pos(r, par, tables=None):
                dve.wait_ge(s["code_done"], r + 1)
                wait(dve, s["tab_done"], r - 1 if tables is None else tables)
                for q in range(GT):
                    last = nc.vector.tensor_tensor(onepos[:, par, q, :, :], iota_c[:, :, :],
                                            pos_h[:, q, 0:TOPK].unsqueeze(1).to_broadcast([P, P, TOPK]),
                                            ALU.is_equal)
                last.then_inc(s["onepos_done"], 1)

            def one_hot_exp(r, par, payloads=None):
                wait(dve, s["payload_done"], r - 1 if payloads is None else payloads)
                for q in range(GT):
                    last = nc.vector.tensor_tensor(oneexp[:, par, q, :, :], iota_e[:, :, :],
                                                   exp_h[:, q, 0:TOPK].unsqueeze(1).to_broadcast([P, E, TOPK]),
                                                   ALU.is_equal)
                last.then_inc(s["oneexp_done"], 1)

            def gated(g, u):
                m = SCH[u // 2][1]
                dve.wait_ge(s["silu_done"], g * UNITS + u + 1)
                wait(dve, s["hTlo_done"], g * UNITS + u - 1)
                wait(dve, s["hThi_done"], g * UNITS + u - 1)
                nc.vector.tensor_tensor(hf[0:m, u % 2, :], sg[0:m, u % 2, :], unit_ps[u % 2][0:m, 1, :],
                                        ALU.mult).then_inc(s["hf_done"], 1)

            def left_of_h(g, u):
                m = SCH[u // 2][1]
                where = (slice(0, m), u // 2, slice((u % 2) * HTOK, (u % 2 + 1) * HTOK))
                dve.wait_ge(s["hThi_done"], g * UNITS + u + 1)
                nc.vector.tensor_tensor(hTlo[where], hf[0:m, u % 2, :], hThi[where].bitcast(F32),
                                        ALU.subtract).then_inc(s["hTlo_done"], 1)

            def add_shared(g):
                for h in range(2):
                    dve.wait_ge(s["z_done"], g * 2 + h + 1)
                    xh = x_all[:, bass.ds(g * GT + 2 * h, 2), :]
                    nc.vector.tensor_tensor(xh, xh, z_ps[h], ALU.add).then_inc(s["zadd_done"], 1)

            dve.wait_ge(s["subj32_done"], 1)
            select(0)
            dve.wait_ge(s["swhi_done"], 1)
            m2 = SCH[2][1]
            nc.vector.tensor_tensor(sw13lo[:, :, :], sw13[:, :, :], sw13hi[:, :, :].bitcast(F32), ALU.subtract)
            nc.vector.tensor_tensor(sw2lo[:, 0:2, :], sw2[:, 0:2, :], sw2hi[:, 0:2, :].bitcast(F32), ALU.subtract)
            nc.vector.tensor_tensor(sw2lo[0:m2, 2, :], sw2[0:m2, 2, :], sw2hi[0:m2, 2, :].bitcast(F32),
                                    ALU.subtract).then_inc(s["swlo_done"], 1)

            def body(b):
                shared = not (isinstance(b, int) and b == 0)
                behind = not (isinstance(b, int) and b <= 1)
                first, second = b * 2, b * 2 + 1
                build_blocks(first, 0)
                build_blocks(second, 1)
                if shared:
                    choose(second - 2, 1)
                    gated(b - 1, 0)
                if behind:
                    one_hot_pos(first - 3, 1, first - 3)
                    one_hot_exp(first - 3, 1, first - 3)
                if shared:
                    sums_of(b - 1)
                    gated(b - 1, 1)
                    slots_of(first - 2)
                    codes_of(first - 2)
                    gated(b - 1, 2)
                shifted_logits(first, 0, b)
                if shared:
                    one_hot_pos(first - 2, 0)
                    gated(b - 1, 3)
                    one_hot_exp(first - 2, 0)
                    slots_of(second - 2)
                    gated(b - 1, 4)
                    codes_of(second - 2)
                    gated(b - 1, 5)
                choose(first, 0)
                select(b + 1)
                shifted_logits(second, 1, b)
                if shared:
                    add_shared(b - 1)

            def read_index(e, slot, rounds):
                wait(dve, xe_in[slot], rounds * 16)
                nc.vector.tensor_copy(ri[:, slot, :], idx_read[:, bass.ds(e, 1)]).then_inc(s["ri_done"], 1)

            def write_index(e, slot):
                wait(dve, acc_added[slot % 2], landed(e, slot))
                nc.vector.tensor_copy(wi[:, slot, :], idx_write[:, bass.ds(e, 1)]).then_inc(s["wi_done"], 1)

            def indices():
                dve.wait_ge(s["tab_final"], 1)
                nc.vector.tensor_scalar(idxf[:, :], tab_ps, float(HALF_N), None, ALU.add).then_inc(s["idxf_done"], 1)
                nc.vector.tensor_scalar(empty[:, :], cnt_ps, iota_p[:, 0:1], dump_p[:, 0:1], ALU.is_le, ALU.mult).then_inc(s["empty_done"], 1)
                dve.wait_ge(s["idxf_done"], 1)
                nc.vector.tensor_copy(idx_read[:, :], idxf[:, :])
                dve.wait_ge(s["empty_done"], 1)
                nc.vector.tensor_tensor(idx_write[:, :], empty[:, :], idxf[:, :], ALU.add).then_inc(s["idx_done"], 1)
                dve.wait_ge(s["idx_done"], 1)

            over_bodies(dve, body)
            g = NB - 1
            choose(NG - 1, 1)
            gated(g, 0)
            one_hot_pos(NG - 3, 1)
            gated(g, 1)
            one_hot_exp(NG - 3, 1)
            slots_of(NG - 2)
            gated(g, 2)
            codes_of(NG - 2)
            gated(g, 3)
            one_hot_pos(NG - 2, 0)
            gated(g, 4)
            one_hot_exp(NG - 2, 0)
            slots_of(NG - 1)
            gated(g, 5)
            codes_of(NG - 1)
            sums_of(NB - 1)
            g = NB
            gated(g, 0)
            one_hot_pos(NG - 1, 1)
            add_shared(g - 1)
            one_hot_exp(NG - 1, 1)
            for u in range(1, 4):
                gated(g, u)
            indices()
            for e in range(SLOTS):
                read_index(e, e, 0)
            write_index(0, 0)
            for u in range(4, UNITS):
                gated(g, u)
            add_shared(g)

            def score_h(e, slot):
                dve.wait_ge(s["eg_done"], e + 1)
                wait(dve, s["eht_done"], e - 1)
                nc.vector.scalar_tensor_tensor(eh[:, slot % 2, :], eg[:, slot % 2, :], xe[:, slot, bass.ds(e + D, 1)],
                                               h_ps[slot % 2][:, INTER:2 * INTER], ALU.mult, ALU.mult).then_inc(s["eh_done"], 1)

            def take_hT(e, slot):
                dve.wait_ge(s["eht_done"], e + 1)
                wait(dve, s["ey_done"], e - 1)
                nc.vector.tensor_copy(ehT[0:IH, slot % 2, :, :], ehT_ps[slot % 2]).then_inc(s["ehT_done"], 1)

            def steady(e, slot, rounds, more=True):
                take_hT(e - 1, (slot - 1) % SLOTS)
                write_index(e, slot)
                score_h(e, slot)
                if more:
                    read_index(e + SLOTS, slot, rounds + 1)

            score_h(0, 0)
            read_index(SLOTS, 0, 1)
            for e in range(1, 1 + SLOTS):
                steady(e, e % SLOTS, e // SLOTS)
            with dve.Fori(1, (E - SLOTS) // SLOTS - 1) as it:
                for j in range(SLOTS):
                    e = 1 + j
                    steady(it * SLOTS + e, e % SLOTS, it + e // SLOTS)
            for e in range(E - 2 * SLOTS + 1, E):
                steady(e, e % SLOTS, e // SLOTS, e < E - SLOTS)
            take_hT(E - 1, (E - 1) % SLOTS)

            def combine(n):
                g = ORDER[n]
                mine = x_all[:, g * GT:(g + 1) * GT, :]
                first, second = acc_sb[0][:, n % BUFS, :, :], acc_sb[1][:, n % BUFS, :, :]
                if g < EARLY:
                    dve.wait_ge(acc_in[n % BUFS], (n // BUFS + 1) * 32)
                    nc.vector.tensor_tensor(mine, first, second, ALU.add).then_inc(s["combined"], 1)
                else:
                    dve.wait_ge(s["sum_done"], sum(i in LATE for i in ORDER[:n + 1]))
                    if AFTER[n][0] > g:
                        dve.wait_ge(s["zadd_done"], g * 2 + 2)
                    nc.vector.tensor_tensor(mine, mine, first, ALU.add).then_inc(s["combined"], 1)

            gated(EARLY, 0)
            left_of_h(EARLY, 0)
            for g in LATE:
                for u in range(1, UNITS):
                    gated(g, u)
                    left_of_h(g, u)
                    for n, after in enumerate(AFTER):
                        if after == (g, u):
                            combine(n)
                if g + 1 < NG:
                    gated(g + 1, 0)
                if AFTER[ORDER.index(g)][0] == g:
                    dve.wait_ge(s["combined"], ORDER.index(g) + 1)
                add_shared(g)
                if g + 1 < NG:
                    left_of_h(g + 1, 0)
            combine(NG - 1)

        @block.tensor
        def _(pe):
            mm = nc.tensor.matmul
            pe.wait_ge(s["consts"], 1)
            mm(tab_ps, zeros_h[:, :], zeros_h[:, 0:E], start=True, stop=False)

            def select_weights(g, par):
                pe.wait_ge(s["sel_done"], g + 1)
                wait(pe, s["ytr_done"], (g - par) * 2)
                for q in range(GT):
                    for h in range(2):
                        for part in range(3):
                            last = mm(selw_ps[par][:, q, :], sel[:, par, h, q * P:(q + 1) * P], tab3[:, h, part, :],
                                      start=(h + part == 0), stop=(h + part == 3))
                last.then_inc(s["selw_done"], 1)

            def rows(g, par, rounds):
                pe.wait_ge(s["wblk_done"], g + 1)
                pe.wait_ge(x_in[par], (rounds + 1) * 16)
                for h in range(2):
                    wait(pe, s["yrow_done"], g * GT + 2 * h - 2)
                    if par == 0:
                        wait(pe, s["zadd_done"], rounds * 2 + h - 3)
                    for q in range(2 * h, 2 * h + 2):
                        last = mm(y_ps[h][:, q % 2, :], wblk[:, par, q, :],
                                  x_all[:, bass.ds(g * GT + q, 1), :].rearrange("p a n -> p (a n)"), start=True, stop=True)
                    last.then_inc(s["y_done"], 1)

            def turn_rows(g, par):
                if par == 0:
                    pe.wait_ge(s["wblk_done"], g + 2)
                for h in range(2):
                    pe.wait_ge(s["yrow_done"], g * GT + 2 * h + 2)
                    wait(pe, s["ytr_done"], g * 2 + h - 1)
                    for q in range(2):
                        for k in range(KD):
                            last = nc.tensor.transpose(yT_ps[h][:, q, k, :], yrow[:, par, 2 * h + q, k * P:(k + 1) * P], ident[:, :])
                    last.then_inc(s["yT_done"], 1)

            def logits(g, par):
                wait(pe, s["shift_done"], g)
                wait(pe, s["slotv_done"], g - 1)
                for q in range(GT):
                    pe.wait_ge(s["ytr_done"], g * 2 + q // 2 + 1)
                    for k in range(KD):
                        last = mm(lg_ps[:, q, :], ytr[:, q, k, :], gate_sb[:, k, :], start=(k == 0), stop=(k == KD - 1))
                last.then_inc(s["lg_done"], 1)

            def positions(r, par):
                pe.wait_ge(s["carry_done"], r + 1)
                if isinstance(r, int) and r == NG - 1:
                    pe.wait_ge(s["slotv_done"], r)
                else:
                    wait(pe, s["shift_done"], r + 2)
                grp = chosen[:, bass.ds(r * GT, GT), :]
                ps = pos_ps
                mm(ps, earlier[:, :], grp, start=True, stop=False)
                mm(ps, mark[:, :], grp, start=False, stop=False)
                for q in range(GT - 1):
                    mm(ps[:, q + 1:GT, :], ones[:, :], chosen[:, bass.ds(r * GT + q, 1), :].to_broadcast([P, GT - 1 - q, E]),
                       start=False, stop=False)
                mm(ps, ones[:, :], carry[:, bass.ds(r, 1), :].to_broadcast([P, GT, E]), start=False, stop=True).then_inc(s["pos_done"], 1)

            def table_of(r, par):
                pe.wait_ge(s["onepos_done"], r + 1)
                pe.wait_ge(s["payload_done"], r + 1)
                for q in range(GT):
                    for k in range(TOPK):
                        last = mm(tab_ps, onepos[:, par, q, :, k], payload[:, par, q, :, k], start=False, stop=False)
                last.then_inc(s["tab_done"], 1)

            def unit(g, u, slot):
                lo, m = SCH[u // 2]
                pe.wait_ge(s["ylo_done"], g + 1)
                wait(pe, s["hf_done"], g * UNITS + u - 1)
                for w in range(2):
                    cols = slice(w * SINTER + lo, w * SINTER + lo + m)
                    n = 0
                    for k in range(KD):
                        for wt, y in ((sw13hi, yhi), (sw13hi, ylo), (sw13lo, yhi)):
                            last = mm(unit_ps[u % 2][0:m, w, :], wt[:, k, cols], y[:, k, bass.ds(slot * GTOK + (u % 2) * HTOK, HTOK)],
                                      start=(n == 0), stop=(n == 3 * KD - 1))
                            n += 1
                last.then_inc(s["unit_done"], 1)

            def down(g, before):
                for h in range(2):
                    wait(pe, s["zadd_done"], g * 2 + h - 1)
                    if before is not None:
                        wait(pe, s["yrow_done"], before * GT + 2 * h + 2)
                    pe.wait_ge(s["hTlo_done"], g * UNITS + (UNITS - 1) + h)
                    for q in range(2):
                        tok = (2 * h + q) * P
                        n = 0
                        for c, (lo, m) in enumerate(SCH):
                            for ht, wt in ((hThi, sw2hi), (hThi, sw2lo), (hTlo, sw2hi)):
                                last = mm(z_ps[h][:, q, :], ht[0:m, c, tok:tok + P], wt[0:m, c, :],
                                          start=(n == 0), stop=(n == 3 * len(SCH) - 1))
                                n += 1
                    last.then_inc(s["z_done"], 1)

            pe.wait_ge(s["tab3_done"], 3)
            pe.wait_ge(s["gate_in"], 16)

            def body(b):
                shared = not (isinstance(b, int) and b == 0)
                behind = not (isinstance(b, int) and b <= 1)
                first, second = b * 2, b * 2 + 1

                def fill(u):
                    if shared:
                        unit(b - 1, u, b - 1)

                select_weights(first, 0)
                select_weights(second, 1)
                fill(0)
                rows(first, 0, b)
                fill(1)
                if shared:
                    positions(first - 2, 0)
                turn_rows(first, 0)
                fill(2)
                logits(first, 0)
                rows(second, 1, b)
                if behind:
                    table_of(first - 3, 1)
                fill(3)
                if shared:
                    positions(second - 2, 1)
                fill(4)
                turn_rows(second, 1)
                fill(5)
                logits(second, 1)
                if shared:
                    down(b - 1, second)
                    table_of(first - 2, 0)

            body(0)
            pe.wait_ge(s["swlo_done"], 1)
            body(1)
            with pe.Fori(2, NB) as b:
                body(b)
            g = NB - 1
            unit(g, 0, g)
            positions(NG - 2, 0)
            unit(g, 1, g)
            unit(g, 2, g)
            unit(g, 3, g)
            positions(NG - 1, 1)
            unit(g, 4, g)
            unit(g, 5, g)
            unit(g + 1, 0, g + 1)
            table_of(NG - 3, 1)
            down(g, None)
            g = NB
            unit(g, 1, g)
            unit(g, 2, g)
            table_of(NG - 2, 0)
            unit(g, 3, g)
            table_of(NG - 1, 1)
            mm(tab_ps, zeros_h[:, :], zeros_h[:, 0:E], start=False, stop=True)
            mm(cnt_ps, ones[:, :], carry[:, NG, :], start=True, stop=True).then_inc(s["tab_final"], 1)
            unit(g, 4, g)
            unit(g, 5, g)
            down(g, None)

            def x_turn(e, slot):
                wait(pe, s["xeT_done"], e - 1)
                for k in range(KD):
                    last = nc.tensor.transpose(xeT_ps[slot % 2][:, k, :], xe[:, slot, k * P:(k + 1) * P], ident[:, :])
                last.then_inc(s["xt_done"], 1)

            def up(e, slot):
                pe.wait_ge(s["xeT_done"], e + 1)
                wait(pe, s["eh_done"], e - 1)
                for k in range(KD):
                    last = mm(h_ps[slot % 2], xeT[:, slot % 2, k, :], w13[:, slot, k, :], start=(k == 0), stop=(k == KD - 1))
                last.then_inc(s["h_done"], 1)

            def h_turn(e, slot):
                pe.wait_ge(s["eh_done"], e + 1)
                wait(pe, s["ehT_done"], e - 1)
                for k in range(2):
                    last = nc.tensor.transpose(ehT_ps[slot % 2][:, k, :], eh[:, slot % 2, k * IH:(k + 1) * IH], ident[:, :])
                last.then_inc(s["eht_done"], 1)

            def down_e(e, slot):
                pe.wait_ge(s["ehT_done"], e + 1)
                wait(pe, s["eyrow_done"], e - 1)
                for k in range(2):
                    last = mm(ey_ps[slot % 2], ehT[0:IH, slot % 2, k, :], w2[:, slot, k, :], start=(k == 0), stop=(k == 1))
                last.then_inc(s["ey_done"], 1)

            def steady(e, slot, rounds, rounds_next):
                pe.wait_ge(xe_in[(slot + 1) % SLOTS], (rounds_next + 1) * 16)
                x_turn(e + 1, (slot + 1) % SLOTS)
                h_turn(e - 1, (slot - 1) % SLOTS)
                pe.wait_ge(w_in[slot], (rounds + 1) * 32)
                up(e, slot)
                down_e(e - 1, (slot - 1) % SLOTS)

            pe.wait_ge(s["hTlo_done"], EARLY * UNITS)
            pe.wait_ge(s["zadd_done"], EARLY * 2)
            pe.wait_ge(s["idx_done"], 1)
            for e in range(2):
                pe.wait_ge(xe_in[e], 16)
                x_turn(e, e)
            pe.wait_ge(w_in[0], 32)
            up(0, 0)
            for e in range(1, 1 + SLOTS):
                steady(e, e % SLOTS, e // SLOTS, (e + 1) // SLOTS)
            with pe.Fori(1, (E - SLOTS) // SLOTS) as it:
                for j in range(SLOTS):
                    e = 1 + j
                    steady(it * SLOTS + e, e % SLOTS, it + e // SLOTS, it + (e + 1) // SLOTS)
            for e in range(E - SLOTS + 1, E - 1):
                steady(e, e % SLOTS, e // SLOTS, (e + 1) // SLOTS)
            e = E - 1
            h_turn(e - 1, (e - 1) % SLOTS)
            pe.wait_ge(w_in[e % SLOTS], E // SLOTS * 32)
            up(e, e % SLOTS)
            down_e(e - 1, (e - 1) % SLOTS)
            h_turn(e, e % SLOTS)
            down_e(e, e % SLOTS)

            pe.wait_ge(s["eh_done"], E)
            pe.wait_ge(s["ehT_done"], E)
            unit(EARLY, 0, EARLY % YSLOTS)
            for g in LATE:
                for u in range(1, UNITS):
                    unit(g, u, g % YSLOTS)
                if g + 1 < NG:
                    unit(g + 1, 0, (g + 1) % YSLOTS)
                down(g, None)


def kernel(x, itok_B_0_7, fside_8xS_0, L0_cond_weights, L0_ffn_gate_w, L0_ffn_w1, L0_ffn_w2, L0_ffn_w3,
           L0_ffn_sw1, L0_ffn_sw2, L0_ffn_sw3):
    import concourse.bacc as bacc
    from concourse.bass_utils import run_bass_kernel_spmd

    w1, w3, w2 = np.asarray(L0_ffn_w1), np.asarray(L0_ffn_w3), np.asarray(L0_ffn_w2)
    up = np.concatenate([w1, w3], axis=1)
    lay = {
        "x": np.asarray(x),
        "subj": np.asarray(itok_B_0_7).reshape(1, B),
        "table": np.concatenate([np.asarray(L0_cond_weights), np.asarray(fside_8xS_0)[:, :, None]], axis=2).reshape(NSUB * C, CW),
        "gate_t": np.asarray(L0_ffn_gate_w).T.reshape(KD, P, E).transpose(1, 0, 2),
        "w13_t": up.transpose(0, 2, 1).reshape(E, KD, P, 2 * INTER).transpose(0, 2, 1, 3),
        "w2_t": w2.transpose(0, 2, 1).reshape(E, 2, IH, D).transpose(0, 2, 1, 3),
        "sw13_t": np.concatenate([np.asarray(L0_ffn_sw1), np.asarray(L0_ffn_sw3)], axis=0).T.reshape(KD, P, 2 * SINTER).transpose(1, 0, 2),
        "sw2_t": np.asarray(L0_ffn_sw2).T,
    }
    nc = bacc.Bacc("TRN2", target_bir_lowering=False, num_devices=1)
    arrays, aps = {}, {}
    for name, a in lay.items():
        a = np.ascontiguousarray(a)
        arrays[name] = a
        aps[name] = nc.dram_tensor(name, a.shape, mybir.dt.from_np(a.dtype), kind="ExternalInput").ap()
    aps["out"] = nc.dram_tensor("out", (B, C, T), F32, kind="ExternalOutput").ap()
    build_adaln_moe(nc, **aps)
    r = run_bass_kernel_spmd(nc, [arrays], core_ids=[0])
    return r.results[0]["out"]
```

```python
import numpy as np
import concourse.bass as bass
from concourse import mybir
from contextlib import ExitStack

F32, I32, BF16, F16 = mybir.dt.float32, mybir.dt.int32, mybir.dt.bfloat16, mybir.dt.float16
F32R = mybir.dt.float32r
ACT, ALU, AX = mybir.ActivationFunctionType, mybir.AluOpType, mybir.AxisListType

B, C, T = 128, 32, 256
NSUB = 8
D = T
E, TOPK, INTER, CAP = 64, 6, 176, 128
SINTER = 2 * INTER
P = 128
N = B * C
NT = N // P
SPT = P // C
KD = D // P
GT = 4
NG = NT // GT
GTOK = GT * P
ROW = D + E
IH = INTER // 2
SCH = [(0, 128), (128, 128), (256, SINTER - 256)]
UNITS = 2 * len(SCH)
HTOK = GTOK // 2
EARLY = 5
NB = NG // 2
YSLOTS = 6
SPG = GTOK // C
SLOTS = 4
BUFS = 5
CW = C + 1
BIG = 3.0e38
GONE = -3.0e38
FLOOR = -87.3
UNCHOSEN = 64 * 128
HALF_N = N // 2


def wait(eng, sem, count):
    if not (isinstance(count, int) and count <= 0):
        eng.wait_ge(sem, count)


def wait_apart(eng, sem, count, passed):
    if not (isinstance(count, int) and count <= 0):
        eng.wait_ge(sem, count)
        eng.sem_inc(passed, 1)


def slot_of(b, par):
    return (2 * b + par) % YSLOTS if isinstance(b, int) else b * -4 + (12 + par)




def build_adaln_moe(nc, x, subj, table, gate_t, w13_t, w2_t, sw13_t, sw2_t, out):
    x_rows = x.rearrange("b c t -> (b c) t").rearrange("(i p) t -> p i t", p=P)
    out_rows = out.rearrange("b c t -> (b c) t").rearrange("(i p) t -> p i t", p=P)

    ctx = ExitStack()
    with ctx:
        def sb(name, shape, dt):
            return ctx.enter_context(nc.sbuf_tensor(name, shape, dt))

        def sem(name):
            return ctx.enter_context(nc.semaphore(name))

        rows_dram = nc.dram_tensor("rows_dram", (N, ROW), F32).ap()
        acc_dram = [nc.dram_tensor(f"acc{a}_dram", (N + CAP, D), F32).ap() for a in range(2)]
        rows_tiles = rows_dram.rearrange("(i p) n -> p i n", p=P)
        acc_tiles = [a[0:N, :].rearrange("(i p) n -> p i n", p=P) for a in acc_dram]

        x_all = sb("x_all", [P, NT, D], F32)
        yhi = sb("yhi", [P, KD, YSLOTS * GTOK], F32R)
        ylo = sb("ylo", [P, KD, YSLOTS * GTOK], F32R)
        sw13hi = sb("sw13hi", [P, KD, 2 * SINTER], F32R)
        sw13lo = sb("sw13lo", [P, KD, 2 * SINTER], F32R)
        sw2hi = sb("sw2hi", [P, len(SCH), D], F32R)
        sw2lo = sb("sw2lo", [P, len(SCH), D], F32R)
        gate_sb = sb("gate_sb", [P, KD, E], F32)
        subj32 = sb("subj32", [P, B + 2 * SPG, 2], BF16)
        table_sb = sb("table_sb", [P, 2, CW], F32)
        tab3 = sb("tab3", [P, 2, 3, CW], BF16)
        tab_left = sb("tab_left", [P, 2, 2, CW], F32)
        rowdiff = sb("rowdiff", [P, 2, C], BF16)
        bias = sb("bias", [P, 2, GT], F32)
        wblk = sb("wblk", [P, 2, GT, P], F32)
        blocks = sb("blocks", [P, SPT, C], F32)
        ytr = sb("ytr", [P, GT, KD, P], F32)
        front = sb("front", [P, max(2 * GT * D + 2 * GTOK, SLOTS * (ROW + D) + 4 * P + 4 * INTER, 4 * GT * D)], F32)
        yrow = front[:, 0:2 * GT * D].rearrange("p (a q n) -> p a q n", a=2, q=GT)
        subj_sb = front[:, 2 * GT * D + 2 * GTOK:2 * GT * D + 2 * GTOK + B].bitcast(I32)
        sel = front[:, 2 * GT * D:2 * GT * D + 2 * GTOK].bitcast(BF16).rearrange("p (a h n) -> p a h n", a=2, h=2)

        def carve(start, *shape):
            size = int(np.prod(shape))
            names = "abc"[:len(shape)]
            v = front[:, start:start + size].rearrange(
                f"p ({' '.join(names)}) -> p {' '.join(names)}", **dict(zip(names, shape)))
            return v, start + size

        xe, at = carve(0, SLOTS, ROW)
        ey, at = carve(at, SLOTS, D)
        ehT, at = carve(at, 2, 2, P)
        eg, at = carve(at, 2, INTER)
        eh, at = carve(at, 2, INTER)
        w_at, x_at = 2 * GTOK, 2 * GTOK + 2 * 2 * INTER
        w13hi, w13lo = [[y[:, :, w_at + i * 2 * INTER:w_at + (i + 1) * 2 * INTER] for i in range(2)] for y in (yhi, ylo)]
        xeThi, xeTlo = [[y[:, :, x_at + i * P:x_at + (i + 1) * P] for i in range(2)] for y in (yhi, ylo)]
        key = sb("key", [P, 2, GT, E + 2], F32)
        left = sb("left", [P, GT, E + 2], F32)
        rowmax = sb("rowmax", [P, GT], F32)
        top8 = sb("top8", [P, GT, 8], F32)
        chosen = sb("chosen", [P, NT, E], BF16)
        pair = sb("pair", [P, 2, E], F32)
        gsum = sb("gsum", [P, E], F32)
        carry = sb("carry", [P, NG + 1, E], BF16)
        exps = sb("exps", [P, 2, GT, E], F32)
        esum = sb("esum", [P, 2, GT], F32)
        rsum = sb("rsum", [P, 2, GT], F32)
        scores = sb("scores", [P, 2, GT, E], F32)
        slot1 = sb("slot1", [P, GT, E], F32)
        slotv = sb("slotv", [P, GT, E], F32)
        s8 = sb("s8", [P, GT, 8], F32)
        slot_i = sb("slot_i", [P, GT, 8], I32)
        pos_i = sb("pos_i", [P, GT, 8], I32)
        exp_i = sb("exp_i", [P, GT, 8], I32)
        pos_h = sb("pos_h", [P, GT, 8], F16)
        exp_h = sb("exp_h", [P, GT, 8], F16)
        back = sb("back", [P, 2 * GT * (P + 2 * E) * TOPK], F16)
        n_pos, n_exp = 2 * GT * P * TOPK, 2 * GT * E * TOPK
        onepos = back[:, 0:n_pos].rearrange("p (a q c k) -> p a q c k", a=2, q=GT, k=TOPK)
        oneexp = back[:, n_pos:n_pos + n_exp].rearrange("p (a q c k) -> p a q c k", a=2, q=GT, k=TOPK)
        payload = back[:, n_pos + n_exp:].rearrange("p (a q c k) -> p a q c k", a=2, q=GT, k=TOPK)
        n_sw13, n_sw2 = 2 * KD * 2 * SINTER, 2 * len(SCH) * D
        sw13 = back[:, 0:n_sw13].bitcast(F32).rearrange("p (k n) -> p k n", k=KD)
        sw2 = back[:, n_sw13:n_sw13 + n_sw2].bitcast(F32).rearrange("p (m n) -> p m n", m=len(SCH))
        in_back = 3
        acc_sb = [[(back[:, (2 * i + a) * 2 * GT * D:(2 * i + a + 1) * 2 * GT * D].bitcast(F32) if i < in_back else
                    front[:, (2 * (i - in_back) + a) * GT * D:(2 * (i - in_back) + a + 1) * GT * D]).rearrange("p (q n) -> p q n", q=GT)
                   for i in range(BUFS)] for a in range(2)]
        idxf = sb("idxf", [P, E], F32)
        empty = sb("empty", [P, E], F32)
        idx_read = sb("idx_read", [P, E], I32)
        idx_write = sb("idx_write", [P, E], I32)
        sg = sb("sg", [P, 2, HTOK], F32)
        hf = sb("hf", [P, 2, HTOK], F32)
        hThi = sb("hThi", [P, len(SCH), GTOK], F32R)
        hTlo = sb("hTlo", [P, len(SCH), GTOK], F32R)
        w13 = sb("w13", [P, SLOTS, KD, 2 * INTER], F32)
        w2 = sb("w2", [IH, SLOTS, 2, D], F32)
        ri = sb("ri", [P, SLOTS, 1], I32)
        wi = sb("wi", [P, SLOTS, 1], I32)
        ident = sb("ident", [P, P], F32)
        earlier = sb("earlier", [P, P], BF16)
        mark = sb("mark", [P, P], BF16)
        ones = sb("ones", [P, P], BF16)
        zeros_h = sb("zeros_h", [P, P], F16)
        zeros = sb("zeros", [P, 1024], F32)
        iota_p = sb("iota_p", [P, 1], F32)
        warm = sb("warm", [P, 1], F32)
        ids_i = sb("ids_i", [P, NT], I32)
        ids = sb("ids", [P, NT], F32)
        dump_p = sb("dump_p", [P, 1], F32)
        slot0 = sb("slot0", [P, E], F32)
        iota_c = sb("iota_c", [P, P, TOPK], F16)
        iota_e = iota_c[:, 0:E, :]

        bank = [ctx.enter_context(nc.psum_tensor(f"bank{i}", [P, 512], F32)) for i in range(8)]

        unit_ps = [bank[i][:, :].rearrange("p (w t) -> p w t", w=2) for i in range(2)]
        selw_ps = [bank[2 + a][:, 0:GT * CW].rearrange("p (q w) -> p q w", q=GT) for a in range(2)]
        yT_ps = [bank[2 + h][:, :].rearrange("p (q k c) -> p q k c", q=2, k=KD) for h in range(2)]
        y_ps = [bank[4 + h][:, :].rearrange("p (q n) -> p q n", q=2) for h in range(2)]
        z_ps = y_ps
        lg_ps = bank[6][:, 0:GT * E].rearrange("p (q e) -> p q e", q=GT)
        pos_ps = lg_ps
        cnt_ps = bank[6][:, 0:E]
        tab_ps = bank[7][:, 0:E]
        xeT_ps = [bank[0 + i][:, 0:D].rearrange("p (k c) -> p k c", k=KD) for i in range(2)]
        h_ps = [bank[2 + i][:, 0:2 * INTER] for i in range(2)]
        ehT_ps = [bank[4 + i][0:IH, 0:2 * P].rearrange("p (k c) -> p k c", k=2) for i in range(2)]
        ey_ps = [bank[6 + i][:, 0:D] for i in range(2)]

        s = {}
        for name in (
            "pool_const", "dve_passed", "pool_passed", "block_zero", "block_one", "ids_done", "consts", "subj_in", "table_in",
            "gate_in", "sw_in", "subj32_done", "tab3_done", "tab_left_done", "sel_done", "selw_done", "bias_done", "wblk_done",
            "swhi_done", "swlo_done",
            "yhi_done", "ylo_done", "hf_done", "hThi_done", "sum_done", "y_done", "yrow_done", "yT_done", "ytr_done", "lg_done",
            "rowmax_done", "shift_done", "key_done", "top8_done", "left_done", "chosen_done", "pair_done", "gsum_done",
            "carry_done", "exp_done", "esum_done", "warm_done", "recip_done", "score_done", "p_stored",
            "pos_done", "slot1_done", "slotv_done", "s8_done", "sloti_done", "split_done", "code_done",
            "onepos_done", "oneexp_done", "payload_done", "tab_done", "tab_final", "idxf_done", "empty_done", "idx_done",
            "unit_done", "silu_done", "z_done", "zadd_done",
            "sums_started", "ri_done", "wi_done", "xt_done", "xhi_done", "xlo_done", "whi_done", "wlo_done", "h_done", "eg_done", "eh_done",
            "eht_done", "ehT_done", "ey_done", "eyrow_done",
            "hTlo_done", "combined", "out_stored",
        ):
            s[name] = sem(name)
        x_in = [sem(f"x_in{i}") for i in range(2)]
        y_stored = [sem(f"y_stored{i}") for i in range(2)]
        w13_in = [sem(f"w13_in{i}") for i in range(SLOTS)]
        w2_in = [sem(f"w2_in{i}") for i in range(SLOTS)]
        xe_in = [sem(f"xe_in{i}") for i in range(SLOTS)]
        acc_added = [sem(f"acc_added{i}") for i in range(2)]
        acc_in = [sem(f"acc_in{i}") for i in range(BUFS)]

        block = ctx.enter_context(nc.Block())

        def over_bodies(eng, body):
            body(0)
            body(1)
            with eng.Fori(2, NB) as b:
                body(b)

        def landed(e, slot):
            if isinstance(e, int):
                return ((e - SLOTS) // 2 + 1) * 16 if e >= SLOTS else 0
            return e * 8 - (SLOTS + slot % 2) * 8 + 16

        LATE = list(range(EARLY, NG))
        PAYS = {(NB - 1, 4): NG - 3, (NB, 0): NG - 2, (NB, 2): NG - 1}
        ORDER = [0, 5, 1, 6, 2, 7, 3, 4]
        ADDS = {(6, 1): 5, (7, 1): 6}

        def free(eng, n):
            if ORDER[n] in LATE:
                eng.wait_ge(s["combined"], LATE.index(ORDER[n]) + 1)
            else:
                eng.wait_ge(s["sum_done"], n + 1)

        @block.sync
        def _(sp):
            sp.dma_start(subj_sb[:, :], subj.to_broadcast([P, B])).then_inc(s["subj_in"], 16)
            sp.dma_start(table_sb[:, :, :], table.rearrange("(h p) w -> p h w", p=P)).then_inc(s["table_in"], 16)
            per = zeros.shape[1] // D
            acc_flat = [acc_dram[a][0:N, :].rearrange("(r p n) d -> r p (n d)", p=P, n=per) for a in range(2)]

            def load_group(g):
                sp.dma_start(x_all[:, g * GT:(g + 1) * GT, :], x_rows[:, g * GT:(g + 1) * GT, :]).then_inc(x_in[g % 2], 16)

            def store_scores(b):
                sp.wait_ge(s["score_done"], b + 1)
                sp.dma_start(rows_tiles[:, 2 * b * GT:2 * (b + 1) * GT, D:ROW],
                             scores.rearrange("p a q e -> p (a q) e")).then_inc(s["p_stored"], 16)

            def start_sum(g):
                sp.wait_ge(s["zadd_done"], g * 2 + 2)
                sp.dma_start(acc_tiles[0][:, g * GT:(g + 1) * GT, :], x_all[:, g * GT:(g + 1) * GT, :]).then_inc(s["sums_started"], 16)

            load_group(0)
            load_group(1)
            sp.dma_start(gate_sb[:, :, :], gate_t).then_inc(s["gate_in"], 16)
            sp.dma_start(sw13[:, :, :], sw13_t).then_inc(s["sw_in"], 16)
            sp.dma_start(sw2[:, 0:2, :], sw2_t[0:2 * P, :].rearrange("(m p) n -> p m n", p=P)).then_inc(s["sw_in"], 16)
            sp.dma_start(sw2[0:SCH[2][1], 2, :], sw2_t[2 * P:SINTER, :]).then_inc(s["sw_in"], 16)
            sp.wait_ge(s["pool_const"], 1)
            for a in range(2):
                sp.dma_start(acc_dram[a][N:N + CAP, :], zeros[:, 0:D]).then_inc(s["sums_started"], 16)
            for g in range(NG):
                if g + 2 < NG:
                    sp.wait_ge(x_in[g % 2], (g // 2 + 1) * 16)
                    load_group(g + 2)
                for a in range(2):
                    if a == 1 or g in LATE:
                        sp.dma_start(acc_flat[a][g], zeros[:, :]).then_inc(s["sums_started"], 16)
                sp.wait_ge(s["yrow_done"], g * GT + GT)
                sp.dma_start(rows_tiles[:, g * GT:(g + 1) * GT, 0:D], yrow[:, g % 2, :, :]).then_inc(y_stored[g % 2], 16)
                if g % 2 == 1 and g > 1:
                    store_scores(g // 2 - 1)
                    if g > 3:
                        start_sum(g // 2 - 2)
            store_scores(NB - 1)

            def load_w13(e, slot):
                wait(sp, s["wlo_done"], (e - SLOTS + 1) * KD)
                sp.dma_start(w13[:, slot, :, :], w13_t[bass.ds(e, 1)].rearrange("a p k n -> p (a k) n")).then_inc(w13_in[slot], 16)

            def load_w2(e, slot):
                wait(sp, s["ey_done"], e - SLOTS + 1)
                sp.dma_start(w2[:, slot, :, :], w2_t[bass.ds(e, 1)].rearrange("a p k n -> p (a k) n")).then_inc(w2_in[slot], 16)

            for slot in range(SLOTS):
                load_w13(slot, slot)
                load_w2(slot, slot)
            for g in range(NB - 2, NB):
                start_sum(g)
            for slot in range(2):
                load_w13(SLOTS + slot, slot)
            start_sum(NB)
            with sp.Fori(1, E // SLOTS - 1) as it:
                for slot in range(SLOTS):
                    load_w2(it * SLOTS + slot, slot)
                    load_w13(it * SLOTS + (slot + 2), (slot + 2) % SLOTS)
            for e in range(E - SLOTS, E):
                load_w2(e, e % SLOTS)
                if e + 2 < E:
                    load_w13(e + 2, (e + 2) % SLOTS)

            def load_sum(n, a):
                g = ORDER[n]
                sp.dma_start(acc_sb[a][n % BUFS], acc_tiles[a][:, g * GT:(g + 1) * GT, :]).then_inc(acc_in[n % BUFS], 16)

            def store_result(g, tiles=range(GT)):
                if g in LATE:
                    sp.wait_ge(s["combined"], LATE.index(g) + 1)
                    sp.wait_ge(s["zadd_done"], g * 2 + tiles[-1] // 2 + 1)
                else:
                    sp.wait_ge(s["sum_done"], ORDER.index(g) + 1)
                i = g * GT + tiles[0]
                sp.dma_start(out_rows[:, i:i + len(tiles), :], x_all[:, i:i + len(tiles), :]).then_inc(s["out_stored"], 16)

            for a in range(2):
                sp.wait_ge(acc_added[a], E // 2 * 16)
                for n in range(1 if a == 0 else BUFS):
                    load_sum(n, a)
                    if a == 1 and n > 0:
                        load_sum(n, 0)
            store_result(0)
            for n, g in ((5, 1), (6, 5), (7, 2)):
                free(sp, n - BUFS)
                for a in range(2):
                    load_sum(n, a)
                store_result(g)
            for g in (6, 3, 4):
                store_result(g)
            for h in range(2):
                store_result(NG - 1, range(2 * h, 2 * h + 2))
            sp.wait_ge(s["out_stored"], (NG + 1) * 16)

        @block.gpsimd
        def _(pool):
            nc.gpsimd.memset(ident[:, :], 1.0)
            nc.gpsimd.memset(earlier[:, :], 1.0)
            nc.gpsimd.memset(mark[:, :], -float(UNCHOSEN))
            nc.gpsimd.memset(ones[:, :], 1.0)
            nc.gpsimd.memset(zeros_h[:, :], 0.0)
            nc.gpsimd.memset(zeros[:, :], 0.0)
            nc.gpsimd.iota(rowdiff[:, :, :], [[P, 2], [-1, C]], base=0, channel_multiplier=1, allow_small_or_imprecise_dtypes=True)
            nc.gpsimd.memset(carry[:, 0, :], 0.0)
            nc.gpsimd.memset(key[:, :, :, E:E + 2], BIG).then_inc(s["pool_const"], 1)
            pool.wait_ge(s["pool_const"], 1)
            nc.gpsimd.affine_select(out=ident[:, :], in_=ident[:, :], compare_op=ALU.is_equal, fill=0.0,
                                    base=0, pattern=[[-1, P]], channel_multiplier=1)
            nc.gpsimd.affine_select(out=mark[:, :], in_=mark[:, :], compare_op=ALU.is_equal, fill=0.0,
                                    base=0, pattern=[[-1, P]], channel_multiplier=1)
            nc.gpsimd.affine_select(out=earlier[:, :], in_=earlier[:, :], compare_op=ALU.is_gt, fill=0.0,
                                    base=0, pattern=[[1, P]], channel_multiplier=-1)
            nc.gpsimd.iota(iota_p[:, :], [[1, 1]], base=0, channel_multiplier=1, allow_small_or_imprecise_dtypes=True)
            nc.gpsimd.iota(dump_p[:, :], [[1, 1]], base=HALF_N, channel_multiplier=1, allow_small_or_imprecise_dtypes=True)
            nc.gpsimd.iota(ids_i[:, :], [[P, NT]], base=-HALF_N, channel_multiplier=1)
            nc.gpsimd.iota(slot0[:, :], [[CAP, E]], base=UNCHOSEN + 1, channel_multiplier=0,
                           allow_small_or_imprecise_dtypes=True)
            nc.gpsimd.iota(iota_c[:, :, :], [[1, P], [0, TOPK]], base=0, channel_multiplier=0,
                           allow_small_or_imprecise_dtypes=True).then_inc(s["consts"], 1)

            def left_of_h(g, u):
                m = SCH[u // 2][1]
                where = (slice(0, m), u // 2, slice((u % 2) * HTOK, (u % 2 + 1) * HTOK))
                pool.wait_ge(s["hThi_done"], g * UNITS + u + 1)
                nc.gpsimd.tensor_tensor(hTlo[where], hf[0:m, u % 2, :], hThi[where].bitcast(F32),
                                        ALU.subtract).then_inc(s["hTlo_done"], 1)

            def carry_of(g):
                pool.wait_ge(s["chosen_done"], g + 1)
                wait(pool, s["carry_done"], g)
                nc.gpsimd.tensor_tensor(pair[:, :, :], chosen[:, g * GT:g * GT + 2, :], chosen[:, g * GT + 2:g * GT + 4, :],
                                        ALU.add).then_inc(s["pair_done"], 1)
                pool.wait_ge(s["pair_done"], g + 1)
                nc.gpsimd.tensor_tensor(gsum[:, :], pair[:, 0, :], pair[:, 1, :], ALU.add).then_inc(s["gsum_done"], 1)
                pool.wait_ge(s["gsum_done"], g + 1)
                nc.gpsimd.tensor_tensor(carry[:, g + 1, :], carry[:, g, :],
                                        gsum[:, :], ALU.add).then_inc(s["carry_done"], 1)

            def scores_of(b):
                pool.wait_ge(s["recip_done"], b + 1)
                wait(pool, s["p_stored"], b * 16)
                nc.gpsimd.tensor_tensor(scores[:, :, :, :], exps[:, :, :, :],
                                        rsum[:, :, :].unsqueeze(3).to_broadcast([P, 2, GT, E]),
                                        ALU.mult).then_inc(s["score_done"], 1)

            def left_of_y(g, slot):
                pool.wait_ge(s["yhi_done"], g + 1)
                for k in range(KD):
                    where = (slice(None), k, slice(slot * GTOK, (slot + 1) * GTOK))
                    last = nc.gpsimd.tensor_tensor(ylo[where].rearrange("p (q c) -> p q c", q=GT), ytr[:, :, k, :],
                                                   yhi[where].bitcast(F32).rearrange("p (q c) -> p q c", q=GT), ALU.subtract)
                last.then_inc(s["ylo_done"], 1)

            for b in range(NB + 1):
                shared, cond = b > 0, b < NB
                if shared:
                    carry_of(b * 2 - 1)
                    left_of_h(b - 1, 0)
                    left_of_h(b - 1, 1)
                if shared and cond:
                    scores_of(b - 1)
                if shared:
                    left_of_h(b - 1, 2)
                if cond:
                    left_of_y(b * 2, (b * 2) % YSLOTS)
                if shared:
                    left_of_h(b - 1, 3)
                    left_of_h(b - 1, 4)
                    left_of_h(b - 1, 5)
                if cond:
                    carry_of(b * 2)
                    left_of_y(b * 2 + 1, (b * 2 + 1) % YSLOTS)

            scores_of(NB - 1)
            for u in range(4):
                left_of_h(NB, u)

            for par in range(2):
                pool.wait_ge(y_stored[par], NG // 2 * 16)
            pool.wait_ge(s["p_stored"], NB * 16)
            pool.wait_ge(s["idx_done"], 1)

            def gather(e, slot, rounds):
                if rounds is not None:
                    pool.wait_ge(s["xt_done"], e - SLOTS + 1)
                    pool.wait_ge(s["eh_done"], e - SLOTS + 1)
                wait_apart(pool, s["ri_done"], e + 1, s["pool_passed"])
                pool.indirect_dma_start(xe[:, slot, :], None, rows_dram, bass.IndirectOffsetOnAxis(ri[:, slot, 0:1], 0),
                                        bounds_check=N - 1, oob_is_err=False).then_inc(xe_in[slot], 16)

            def scatter(e, slot):
                a = slot % 2
                wait(pool, acc_added[a], (e - slot) // 2 * 16 + slot // 2 * 16 if isinstance(e, int) else e * 8 - a * 8)
                wait_apart(pool, s["wi_done"], e + 1, s["pool_passed"])
                wait_apart(pool, s["eyrow_done"], e + 1, s["pool_passed"])
                pool.indirect_dma_start(acc_dram[a], bass.IndirectOffsetOnAxis(wi[:, slot, 0:1], 0), ey[:, slot, :], None,
                                        bounds_check=N + CAP - 1, oob_is_err=True, compute_op=ALU.add).then_inc(acc_added[a], 16)

            for slot in range(SLOTS):
                gather(slot, slot, None)
            for slot in range(SLOTS):
                gather(SLOTS + slot, slot, 1)
                if slot == 0:
                    pool.wait_ge(s["sums_started"], 2 * (NG + 1) * 16)
                scatter(slot, slot)
            with pool.Fori(1, E // SLOTS - 1) as it:
                for slot in range(SLOTS):
                    gather(it * SLOTS + (SLOTS + slot), slot, it + 1)
                    scatter(it * SLOTS + slot, slot)
            for slot in range(SLOTS):
                scatter(E - SLOTS + slot, slot)

            for n, g in enumerate(ORDER):
                first, second = acc_sb[0][n % BUFS], acc_sb[1][n % BUFS]
                pool.wait_ge(acc_in[n % BUFS], (n // BUFS + 1) * 32)
                nc.gpsimd.tensor_tensor(first if g in LATE else x_all[:, g * GT:(g + 1) * GT, :], first, second,
                                        ALU.add).then_inc(s["sum_done"], 1)

        @block.scalar
        def _(act):
            def load_table(function, before):
                wait(act, s["warm_done"], before)
                nc.scalar.activation(warm[:, :], zeros[:, 0:1], function).then_inc(s["warm_done"], 1)

            act.wait_ge(s["pool_const"], 1)
            load_table(ACT.Exp, 0)

            def round_shared_weights():
                act.wait_ge(s["sw_in"], 48)
                nc.scalar.copy(sw13hi[:, :, :], sw13[:, :, :])
                nc.scalar.copy(sw2hi[:, 0:2, :], sw2[:, 0:2, :])
                nc.scalar.copy(sw2hi[0:SCH[2][1], 2, :], sw2[0:SCH[2][1], 2, :]).then_inc(s["swhi_done"], 1)

            def take_rows(g, par, rounds):
                act.wait_ge(s["bias_done"], g + 1)
                wait(act, y_stored[par], rounds * 16)
                for q in range(GT):
                    act.wait_ge(s["y_done"], g * 2 + q // 2 + 1)
                    nc.scalar.activation(yrow[:, par, q, :], y_ps[q // 2][:, q % 2, :], ACT.Identity,
                                         bias=bias[:, par, q:q + 1]).then_inc(s["yrow_done"], 1)

            def take_yT(g):
                wait(act, s["lg_done"], g)
                wait(act, s["ylo_done"], g)
                for h in range(2):
                    act.wait_ge(s["yT_done"], g * 2 + h + 1)
                    nc.scalar.copy(ytr[:, 2 * h:2 * h + 2, :, :], yT_ps[h]).then_inc(s["ytr_done"], 1)

            def round_y(g, slot, b):
                act.wait_ge(s["ytr_done"], g * 2 + 2)
                wait(act, s["unit_done"], b * UNITS - UNITS)
                for k in range(KD):
                    last = nc.scalar.copy(yhi[:, k, bass.ds(slot * GTOK, GTOK)].rearrange("p (q c) -> p q c", q=GT), ytr[:, :, k, :])
                last.then_inc(s["yhi_done"], 1)

            def exp_of(b):
                load_table(ACT.Exp, b * 2 + 1)
                act.wait_ge(s["key_done"], b * 2 + 2)
                wait(act, s["score_done"], b)
                nc.scalar.activation(exps[:, :, :, :], key[:, :, :, 0:E], ACT.Exp).then_inc(s["exp_done"], 1)
                load_table(ACT.Silu, b * 2 + 2)

            def silu(g, u):
                m = SCH[u // 2][1]
                act.wait_ge(s["unit_done"], g * UNITS + u + 1)
                wait(act, s["hf_done"], g * UNITS + u - 1)
                nc.scalar.activation(sg[0:m, u % 2, :], unit_ps[u % 2][0:m, 0, :], ACT.Silu).then_inc(s["silu_done"], 1)

            def round_h(g, u):
                m = SCH[u // 2][1]
                act.wait_ge(s["hf_done"], g * UNITS + u + 1)
                wait(act, s["z_done"], g * 2)
                nc.scalar.copy(hThi[0:m, u // 2, (u % 2) * HTOK:(u % 2 + 1) * HTOK], hf[0:m, u % 2, :]).then_inc(s["hThi_done"], 1)

            def pay(r, par, tables=None):
                if isinstance(r, int) and r == 0:
                    act.wait_ge(s["ids_done"], 1)
                act.wait_ge(s["oneexp_done"], r + 1)
                wait(act, s["tab_done"], r - 1 if tables is None else tables)
                for q in range(GT):
                    last = nc.scalar.activation(payload[:, par, q, :, :], oneexp[:, par, q, :, :], ACT.Copy,
                                                scale=ids[:, bass.ds(r * GT + q, 1)])
                last.then_inc(s["payload_done"], 1)

            def body(b):
                shared = not (isinstance(b, int) and b == 0)
                behind = not (isinstance(b, int) and b <= 1)
                if shared:
                    silu(b - 1, 0)
                    round_h(b - 1, 0)
                take_rows(b * 2, 0, b)
                if not shared:
                    round_shared_weights()
                if shared:
                    silu(b - 1, 1)
                    round_h(b - 1, 1)
                take_yT(b * 2)
                round_y(b * 2, slot_of(b, 0), b)
                if behind:
                    pay(b * 2 - 3, 1, b * 2 - 3)
                if shared:
                    silu(b - 1, 2)
                    round_h(b - 1, 2)
                    silu(b - 1, 3)
                take_rows(b * 2 + 1, 1, b)
                if shared:
                    round_h(b - 1, 3)
                    silu(b - 1, 4)
                take_yT(b * 2 + 1)
                if shared:
                    round_h(b - 1, 4)
                    silu(b - 1, 5)
                round_y(b * 2 + 1, slot_of(b, 1), b)
                if shared:
                    round_h(b - 1, 5)
                    pay(b * 2 - 2, 0)
                exp_of(b)

            over_bodies(act, body)

            def round_w(e, slot, rounds):
                act.wait_ge(w13_in[slot], (rounds + 1) * 16)
                wait(act, s["h_done"], e - 1)
                nc.scalar.copy(w13hi[slot % 2], w13[:, slot, :, :]).then_inc(s["whi_done"], 1)

            for g in (NB - 1, NB):
                for u in range(UNITS):
                    silu(g, u)
                    if g == NB and u >= 4:
                        act.wait_ge(s["unit_done"], NB * UNITS)
                        round_w(u - 4, u - 4, 0)
                    if (g, u) in PAYS:
                        pay(PAYS[g, u], PAYS[g, u] % 2)
                    round_h(g, u)

            def take_xT(e, slot):
                act.wait_ge(s["xt_done"], e + 1)
                wait(act, s["h_done"], e - 1)
                nc.scalar.copy(xeThi[slot % 2], xeT_ps[slot % 2]).then_inc(s["xhi_done"], 1)

            def take_h(e, slot):
                act.wait_ge(s["h_done"], e + 1)
                wait(act, s["eh_done"], e - 1)
                nc.scalar.activation(eg[:, slot % 2, :], h_ps[slot % 2][:, 0:INTER], ACT.Silu).then_inc(s["eg_done"], 1)

            def take_y(e, slot):
                act.wait_ge(s["ey_done"], e + 1)
                wait(act, acc_added[slot % 2], landed(e, slot))
                nc.scalar.copy(ey[:, slot, :], ey_ps[slot % 2]).then_inc(s["eyrow_done"], 1)

            def steady(e, slot, rounds):
                take_xT(e + 1, slot + 1)
                round_w(e + 1, (slot + 1) % SLOTS, rounds)
                take_h(e, slot)
                take_y(e - 1, (slot - 1) % SLOTS)

            take_xT(0, 0)
            take_xT(1, 1)
            take_h(0, 0)
            for e in range(1, 1 + SLOTS):
                steady(e, e % SLOTS, (e + 1) // SLOTS)
            with act.Fori(1, (E - SLOTS) // SLOTS) as it:
                for j in range(SLOTS):
                    steady(it * SLOTS + (1 + j), (1 + j) % SLOTS, it + (2 + j) // SLOTS)
            for e in range(E - SLOTS + 1, E - 1):
                steady(e, e % SLOTS, (e + 1) // SLOTS)
            take_h(E - 1, (E - 1) % SLOTS)
            take_y(E - 2, (E - 2) % SLOTS)
            take_y(E - 1, (E - 1) % SLOTS)

            for g in LATE:
                silu(g, 0)
                for u in range(1, UNITS):
                    silu(g, u)
                    round_h(g, u - 1)
                round_h(g, UNITS - 1)

        @block.vector
        def _(dve):
            nc.vector.memset(blocks[:, :, :], 0.0).then_inc(s["block_zero"], 1)
            dve.wait_ge(s["block_zero"], 1)
            for j in range(SPT):
                last = nc.vector.memset(blocks[j * C:(j + 1) * C, j, :], 1.0)
            last.then_inc(s["block_one"], 1)
            dve.wait_ge(s["block_one"], 1)
            dve.wait_ge(s["subj_in"], 16)
            nc.vector.memset(subj32[:, B:, :], 0.0)
            nc.vector.tensor_scalar(subj32[:, 0:B, :], subj_sb[:, :].unsqueeze(2).to_broadcast([P, B, 2]), float(C), None,
                                    ALU.mult).then_inc(s["subj32_done"], 1)
            dve.wait_ge(s["table_in"], 16)
            nc.vector.tensor_copy(tab3[:, :, 0, :], table_sb[:, :, :]).then_inc(s["tab3_done"], 1)
            dve.wait_ge(s["tab3_done"], 1)
            nc.vector.tensor_tensor(tab_left[:, 0, :, :], table_sb[:, :, :], tab3[:, :, 0, :], ALU.subtract).then_inc(s["tab_left_done"], 1)
            dve.wait_ge(s["tab_left_done"], 1)
            nc.vector.tensor_copy(tab3[:, :, 1, :], tab_left[:, 0, :, :]).then_inc(s["tab3_done"], 1)
            dve.wait_ge(s["tab3_done"], 2)
            nc.vector.tensor_tensor(tab_left[:, 1, :, :], tab_left[:, 0, :, :], tab3[:, :, 1, :], ALU.subtract).then_inc(s["tab_left_done"], 1)
            dve.wait_ge(s["tab_left_done"], 2)
            nc.vector.tensor_copy(tab3[:, :, 2, :], tab_left[:, 1, :, :]).then_inc(s["tab3_done"], 1)

            def build_blocks(g, par):
                dve.wait_ge(s["selw_done"], g + 1)
                wait(dve, s["yrow_done"], (g - 1) * GT)
                nc.vector.tensor_copy(bias[:, par, :], selw_ps[par][:, :, C]).then_inc(s["bias_done"], 1)
                nc.vector.tensor_tensor(wblk[:, par, :, :].rearrange("p q (j d) -> p q j d", j=SPT),
                                        selw_ps[par][:, :, 0:C].unsqueeze(2).to_broadcast([P, GT, SPT, C]),
                                        blocks[:, :, :].unsqueeze(1).to_broadcast([P, GT, SPT, C]),
                                        ALU.mult).then_inc(s["wblk_done"], 1)

            def select(b):
                wait(dve, s["selw_done"], b * 2)
                for par in range(2):
                    for h in range(2):
                        last = nc.vector.tensor_tensor(
                            sel[:, par, h, :].rearrange("p (s c e) -> p s c e", c=C // 2, e=2),
                            subj32[:, bass.ds(b * (2 * SPG) + par * SPG, SPG), :].unsqueeze(2).to_broadcast([P, SPG, C // 2, 2]),
                            rowdiff[:, h, :].rearrange("p (c e) -> p c e", e=2).unsqueeze(1).to_broadcast([P, SPG, C // 2, 2]),
                            ALU.is_equal)
                    last.then_inc(s["sel_done"], 1)

            def shifted_logits(g, par, b):
                dve.wait_ge(s["lg_done"], g + 1)
                nc.vector.tensor_reduce(rowmax[:, :], lg_ps, AX.X, ALU.max).then_inc(s["rowmax_done"], 1)
                dve.wait_ge(s["rowmax_done"], g + 1)
                wait(dve, s["exp_done"], b)
                k64 = key[:, par, :, 0:E]
                nc.vector.tensor_tensor(k64, lg_ps, rowmax[:, :].unsqueeze(2).to_broadcast([P, GT, E]),
                                        ALU.subtract).then_inc(s["shift_done"], 1)
                dve.wait_ge(s["shift_done"], g + 1)
                nc.vector.tensor_scalar(k64, k64, FLOOR, None, ALU.max).then_inc(s["key_done"], 1)

            def choose(g, par):
                wait_apart(dve, s["key_done"], g + 1, s["dve_passed"])
                for q in range(GT):
                    last = nc.vector.max(top8[:, q, :], key[:, par, q, :])
                last.then_inc(s["top8_done"], 1)
                wait_apart(dve, s["top8_done"], g + 1, s["dve_passed"])
                for q in range(GT):
                    last = nc.vector.match_replace(left[:, q, :], top8[:, q, :], key[:, par, q, :], GONE)
                last.then_inc(s["left_done"], 1)
                dve.wait_ge(s["left_done"], g + 1)
                mine = chosen[:, bass.ds(g * GT, GT), :]
                nc.vector.tensor_tensor(mine, left[:, :, 0:E], key[:, par, :, 0:E], ALU.is_lt).then_inc(s["chosen_done"], 1)

            def sums_of(b):
                dve.wait_ge(s["exp_done"], b + 1)
                nc.vector.tensor_reduce(esum[:, :, :], exps[:, :, :, :], AX.X, ALU.add).then_inc(s["esum_done"], 1)
                dve.wait_ge(s["esum_done"], b + 1)
                wait(dve, s["score_done"], b)
                nc.vector.reciprocal(rsum[:, :, :], esum[:, :, :]).then_inc(s["recip_done"], 1)

            def slots_of(r):
                dve.wait_ge(s["pos_done"], r + 1)
                nc.vector.tensor_tensor(slot1[:, :, :], pos_ps, slot0[:, :].unsqueeze(1).to_broadcast([P, GT, E]),
                                        ALU.add).then_inc(s["slot1_done"], 1)
                dve.wait_ge(s["slot1_done"], r + 1)
                nc.vector.scalar_tensor_tensor(slotv[:, :, :], pos_ps, float(CAP - UNCHOSEN), slot1[:, :, :],
                                               ALU.is_lt, ALU.mult).then_inc(s["slotv_done"], 1)

            def codes_of(r):
                wait_apart(dve, s["slotv_done"], r + 1, s["dve_passed"])
                for q in range(GT):
                    last = nc.vector.max(s8[:, q, :], slotv[:, q, :])
                last.then_inc(s["s8_done"], 1)
                dve.wait_ge(s["s8_done"], r + 1)
                nc.vector.tensor_scalar(slot_i[:, :, :], s8[:, :, :], -1.0, None, ALU.add).then_inc(s["sloti_done"], 1)
                dve.wait_ge(s["sloti_done"], r + 1)
                nc.vector.tensor_scalar(pos_i[:, :, :], slot_i[:, :, :], CAP - 1, None, ALU.bitwise_and)
                nc.vector.tensor_scalar(exp_i[:, :, :], slot_i[:, :, :], 7, None, ALU.arith_shift_right).then_inc(s["split_done"], 1)
                dve.wait_ge(s["split_done"], r + 1)
                nc.vector.tensor_copy(pos_h[:, :, :], pos_i[:, :, :])
                nc.vector.tensor_copy(exp_h[:, :, :], exp_i[:, :, :]).then_inc(s["code_done"], 1)

            def one_hot_pos(r, par, tables=None):
                dve.wait_ge(s["code_done"], r + 1)
                wait(dve, s["tab_done"], r - 1 if tables is None else tables)
                for q in range(GT):
                    last = nc.vector.tensor_tensor(onepos[:, par, q, :, :], iota_c[:, :, :],
                                            pos_h[:, q, 0:TOPK].unsqueeze(1).to_broadcast([P, P, TOPK]),
                                            ALU.is_equal)
                last.then_inc(s["onepos_done"], 1)

            def one_hot_exp(r, par, payloads=None):
                wait(dve, s["payload_done"], r - 1 if payloads is None else payloads)
                for q in range(GT):
                    last = nc.vector.tensor_tensor(oneexp[:, par, q, :, :], iota_e[:, :, :],
                                                   exp_h[:, q, 0:TOPK].unsqueeze(1).to_broadcast([P, E, TOPK]),
                                                   ALU.is_equal)
                last.then_inc(s["oneexp_done"], 1)

            def gated(g, u):
                m = SCH[u // 2][1]
                dve.wait_ge(s["silu_done"], g * UNITS + u + 1)
                wait(dve, s["hTlo_done"], g * UNITS + u - 1)
                wait(dve, s["hThi_done"], g * UNITS + u - 1)
                nc.vector.tensor_tensor(hf[0:m, u % 2, :], sg[0:m, u % 2, :], unit_ps[u % 2][0:m, 1, :],
                                        ALU.mult).then_inc(s["hf_done"], 1)

            def left_of_h(g, u):
                m = SCH[u // 2][1]
                where = (slice(0, m), u // 2, slice((u % 2) * HTOK, (u % 2 + 1) * HTOK))
                dve.wait_ge(s["hThi_done"], g * UNITS + u + 1)
                nc.vector.tensor_tensor(hTlo[where], hf[0:m, u % 2, :], hThi[where].bitcast(F32),
                                        ALU.subtract).then_inc(s["hTlo_done"], 1)

            def add_half(g, h):
                dve.wait_ge(s["z_done"], g * 2 + h + 1)
                xh = x_all[:, bass.ds(g * GT + 2 * h, 2), :]
                nc.vector.tensor_tensor(xh, xh, z_ps[h], ALU.add).then_inc(s["zadd_done"], 1)

            def add_shared(g):
                for h in range(2):
                    add_half(g, h)

            dve.wait_ge(s["subj32_done"], 1)
            dve.wait_ge(s["pool_const"], 1)
            select(0)

            def split_shared_weights():
                dve.wait_ge(s["swhi_done"], 1)
                m2 = SCH[2][1]
                nc.vector.tensor_tensor(sw13lo[:, :, :], sw13[:, :, :], sw13hi[:, :, :].bitcast(F32), ALU.subtract)
                nc.vector.tensor_tensor(sw2lo[:, 0:2, :], sw2[:, 0:2, :], sw2hi[:, 0:2, :].bitcast(F32), ALU.subtract)
                nc.vector.tensor_tensor(sw2lo[0:m2, 2, :], sw2[0:m2, 2, :], sw2hi[0:m2, 2, :].bitcast(F32),
                                        ALU.subtract).then_inc(s["swlo_done"], 1)
                dve.wait_ge(s["consts"], 1)
                nc.vector.tensor_copy(ids[:, :], ids_i[:, :]).then_inc(s["ids_done"], 1)

            def body(b):
                shared = not (isinstance(b, int) and b == 0)
                behind = not (isinstance(b, int) and b <= 1)
                first, second = b * 2, b * 2 + 1
                build_blocks(first, 0)
                build_blocks(second, 1)
                if not shared:
                    split_shared_weights()
                if shared:
                    choose(second - 2, 1)
                    gated(b - 1, 0)
                if behind:
                    one_hot_pos(first - 3, 1, first - 3)
                if shared:
                    gated(b - 1, 1)
                    slots_of(first - 2)
                if behind:
                    one_hot_exp(first - 3, 1, first - 3)
                if shared:
                    sums_of(b - 1)
                    codes_of(first - 2)
                    gated(b - 1, 2)
                shifted_logits(first, 0, b)
                if shared:
                    one_hot_pos(first - 2, 0)
                    gated(b - 1, 3)
                    slots_of(second - 2)
                    one_hot_exp(first - 2, 0)
                    gated(b - 1, 4)
                    codes_of(second - 2)
                    gated(b - 1, 5)
                choose(first, 0)
                select(b + 1)
                shifted_logits(second, 1, b)
                if shared:
                    add_shared(b - 1)

            def left_of_w(e, slot, k):
                dve.wait_ge(s["whi_done"], e + 1)
                nc.vector.tensor_tensor(w13lo[slot % 2][:, k, :], w13[:, slot, k, :], w13hi[slot % 2].bitcast(F32)[:, k, :],
                                        ALU.subtract).then_inc(s["wlo_done"], 1)

            def read_index(e, slot, rounds):
                wait(dve, xe_in[slot], rounds * 16)
                nc.vector.tensor_copy(ri[:, slot, :], idx_read[:, bass.ds(e, 1)]).then_inc(s["ri_done"], 1)

            def write_index(e, slot):
                wait(dve, acc_added[slot % 2], landed(e, slot))
                nc.vector.tensor_copy(wi[:, slot, :], idx_write[:, bass.ds(e, 1)]).then_inc(s["wi_done"], 1)

            def indices():
                dve.wait_ge(s["tab_final"], 1)
                nc.vector.tensor_scalar(idxf[:, :], tab_ps, float(HALF_N), None, ALU.add).then_inc(s["idxf_done"], 1)
                nc.vector.tensor_scalar(empty[:, :], cnt_ps, iota_p[:, 0:1], dump_p[:, 0:1], ALU.is_le, ALU.mult).then_inc(s["empty_done"], 1)
                dve.wait_ge(s["idxf_done"], 1)
                nc.vector.tensor_copy(idx_read[:, :], idxf[:, :])
                dve.wait_ge(s["empty_done"], 1)
                nc.vector.tensor_tensor(idx_write[:, :], empty[:, :], idxf[:, :], ALU.add).then_inc(s["idx_done"], 1)
                dve.wait_ge(s["idx_done"], 1)

            over_bodies(dve, body)
            g = NB - 1
            choose(NG - 1, 1)
            gated(g, 0)
            one_hot_pos(NG - 3, 1)
            gated(g, 1)
            one_hot_exp(NG - 3, 1)
            slots_of(NG - 2)
            gated(g, 2)
            codes_of(NG - 2)
            gated(g, 3)
            one_hot_pos(NG - 2, 0)
            gated(g, 4)
            one_hot_exp(NG - 2, 0)
            slots_of(NG - 1)
            gated(g, 5)
            codes_of(NG - 1)
            sums_of(NB - 1)
            g = NB
            gated(g, 0)
            one_hot_pos(NG - 1, 1)
            add_shared(g - 1)
            one_hot_exp(NG - 1, 1)
            for u in range(1, 4):
                gated(g, u)
            indices()
            for e in range(SLOTS):
                read_index(e, e, 0)
            write_index(0, 0)
            for u in range(4, UNITS):
                gated(g, u)
                dve.wait_ge(s["hTlo_done"], g * UNITS + 4)
                left_of_h(g, u)
            for e in range(2):
                for k in range(KD):
                    left_of_w(e, e, k)
            add_half(g, 0)

            def left_of_x(e, slot):
                dve.wait_ge(s["xhi_done"], e + 1)
                nc.vector.tensor_tensor(xeTlo[slot % 2], xeT_ps[slot % 2], xeThi[slot % 2].bitcast(F32),
                                        ALU.subtract).then_inc(s["xlo_done"], 1)

            def score_h(e, slot):
                dve.wait_ge(s["eg_done"], e + 1)
                wait(dve, s["eht_done"], e - 1)
                nc.vector.scalar_tensor_tensor(eh[:, slot % 2, :], eg[:, slot % 2, :], xe[:, slot, bass.ds(e + D, 1)],
                                               h_ps[slot % 2][:, INTER:2 * INTER], ALU.mult, ALU.mult).then_inc(s["eh_done"], 1)

            def take_hT(e, slot):
                dve.wait_ge(s["eht_done"], e + 1)
                wait(dve, s["ey_done"], e - 1)
                nc.vector.tensor_copy(ehT[0:IH, slot % 2, :, :], ehT_ps[slot % 2]).then_inc(s["ehT_done"], 1)

            def steady(e, slot, rounds, more=True, following=True):
                take_hT(e - 1, (slot - 1) % SLOTS)
                if following:
                    left_of_x(e + 1, (slot + 1) % SLOTS)
                    left_of_w(e + 1, (slot + 1) % SLOTS, 0)
                write_index(e, slot)
                score_h(e, slot)
                if following:
                    left_of_w(e + 1, (slot + 1) % SLOTS, 1)
                if more:
                    read_index(e + SLOTS, slot, rounds + 1)

            left_of_x(0, 0)
            left_of_x(1, 1)
            add_half(NB, 1)
            score_h(0, 0)
            read_index(SLOTS, 0, 1)
            for e in range(1, 1 + SLOTS):
                steady(e, e % SLOTS, e // SLOTS)
            with dve.Fori(1, (E - SLOTS) // SLOTS - 1) as it:
                for j in range(SLOTS):
                    e = 1 + j
                    steady(it * SLOTS + e, e % SLOTS, it + e // SLOTS)
            for e in range(E - 2 * SLOTS + 1, E):
                steady(e, e % SLOTS, e // SLOTS, e < E - SLOTS, e + 1 < E)
            take_hT(E - 1, (E - 1) % SLOTS)

            def combine(g):
                mine = x_all[:, g * GT:(g + 1) * GT, :]
                dve.wait_ge(s["sum_done"], ORDER.index(g) + 1)
                dve.wait_ge(s["zadd_done"], (g if g == NG - 1 else g + 1) * 2)
                nc.vector.tensor_tensor(mine, mine, acc_sb[0][ORDER.index(g) % BUFS], ALU.add).then_inc(s["combined"], 1)

            gated(EARLY, 0)
            for g in LATE:
                for u in range(1, UNITS):
                    gated(g, u)
                    left_of_h(g, u - 1)
                    if (g, u) in ADDS:
                        combine(ADDS[g, u])
                left_of_h(g, UNITS - 1)
                if g + 1 < NG:
                    gated(g + 1, 0)
                else:
                    combine(g)
                    dve.wait_ge(s["combined"], len(LATE))
                add_shared(g)

        @block.tensor
        def _(pe):
            mm = nc.tensor.matmul
            pe.wait_ge(s["pool_const"], 1)
            mm(tab_ps, zeros_h[:, :], zeros_h[:, 0:E], start=True, stop=False)

            def select_weights(g, par):
                pe.wait_ge(s["sel_done"], g + 1)
                wait(pe, s["ytr_done"], (g - par) * 2)
                for q in range(GT):
                    for h in range(2):
                        for part in range(3):
                            last = mm(selw_ps[par][:, q, :], sel[:, par, h, q * P:(q + 1) * P], tab3[:, h, part, :],
                                      start=(h + part == 0), stop=(h + part == 3))
                last.then_inc(s["selw_done"], 1)

            def rows(g, par, rounds):
                pe.wait_ge(s["wblk_done"], g + 1)
                pe.wait_ge(x_in[par], (rounds + 1) * 16)
                for h in range(2):
                    wait(pe, s["yrow_done"], g * GT + 2 * h - 2)
                    if par == 0:
                        wait(pe, s["zadd_done"], rounds * 2 + h - 3)
                    for q in range(2 * h, 2 * h + 2):
                        last = mm(y_ps[h][:, q % 2, :], wblk[:, par, q, :],
                                  x_all[:, bass.ds(g * GT + q, 1), :].rearrange("p a n -> p (a n)"), start=True, stop=True)
                    last.then_inc(s["y_done"], 1)

            def turn_rows(g, par):
                if par == 0:
                    pe.wait_ge(s["wblk_done"], g + 2)
                for h in range(2):
                    pe.wait_ge(s["yrow_done"], g * GT + 2 * h + 2)
                    wait(pe, s["ytr_done"], g * 2 + h - 1)
                    for q in range(2):
                        for k in range(KD):
                            last = nc.tensor.transpose(yT_ps[h][:, q, k, :], yrow[:, par, 2 * h + q, k * P:(k + 1) * P], ident[:, :])
                    last.then_inc(s["yT_done"], 1)

            def logits(g, par):
                if isinstance(g, int) and g == 0:
                    pe.wait_ge(s["gate_in"], 16)
                wait(pe, s["shift_done"], g)
                wait(pe, s["slotv_done"], g - 1)
                for q in range(GT):
                    pe.wait_ge(s["ytr_done"], g * 2 + q // 2 + 1)
                    for k in range(KD):
                        last = mm(lg_ps[:, q, :], ytr[:, q, k, :], gate_sb[:, k, :], start=(k == 0), stop=(k == KD - 1))
                last.then_inc(s["lg_done"], 1)

            def positions(r, par):
                pe.wait_ge(s["carry_done"], r + 1)
                if isinstance(r, int) and r == NG - 1:
                    pe.wait_ge(s["slotv_done"], r)
                else:
                    wait(pe, s["shift_done"], r + 2)
                grp = chosen[:, bass.ds(r * GT, GT), :]
                mm(pos_ps, earlier[:, :], grp, start=True, stop=False)
                mm(pos_ps, mark[:, :], grp, start=False, stop=False)
                for q in range(GT - 1):
                    mm(pos_ps[:, q + 1:GT, :], ones[:, :], chosen[:, bass.ds(r * GT + q, 1), :].to_broadcast([P, GT - 1 - q, E]),
                       start=False, stop=False)
                mm(pos_ps, ones[:, :], carry[:, bass.ds(r, 1), :].to_broadcast([P, GT, E]), start=False, stop=True).then_inc(s["pos_done"], 1)

            def table_of(r, par):
                pe.wait_ge(s["onepos_done"], r + 1)
                pe.wait_ge(s["payload_done"], r + 1)
                for q in range(GT):
                    for k in range(TOPK):
                        last = mm(tab_ps, onepos[:, par, q, :, k], payload[:, par, q, :, k], start=False, stop=False)
                last.then_inc(s["tab_done"], 1)

            def unit(g, u, slot):
                lo, m = SCH[u // 2]
                pe.wait_ge(s["ylo_done"], g + 1)
                wait(pe, s["hf_done"], g * UNITS + u - 1)
                for w in range(2):
                    cols = slice(w * SINTER + lo, w * SINTER + lo + m)
                    n = 0
                    for k in range(KD):
                        for wt, y in ((sw13hi, yhi), (sw13hi, ylo), (sw13lo, yhi)):
                            last = mm(unit_ps[u % 2][0:m, w, :], wt[:, k, cols], y[:, k, bass.ds(slot * GTOK + (u % 2) * HTOK, HTOK)],
                                      start=(n == 0), stop=(n == 3 * KD - 1))
                            n += 1
                last.then_inc(s["unit_done"], 1)

            def down_half(g, h, before):
                wait(pe, s["zadd_done"], g * 2 + h - 1)
                if before is not None:
                    wait(pe, s["yrow_done"], before * GT + 2 * h + 2)
                pe.wait_ge(s["hTlo_done"], g * UNITS + (UNITS - 1) + h)
                for q in range(2):
                    tok = (2 * h + q) * P
                    n = 0
                    for c, (lo, m) in enumerate(SCH):
                        for ht, wt in ((hThi, sw2hi), (hThi, sw2lo), (hTlo, sw2hi)):
                            last = mm(z_ps[h][:, q, :], ht[0:m, c, tok:tok + P], wt[0:m, c, :],
                                      start=(n == 0), stop=(n == 3 * len(SCH) - 1))
                            n += 1
                last.then_inc(s["z_done"], 1)

            def down(g, before):
                for h in range(2):
                    down_half(g, h, before)

            def body(b):
                shared = not (isinstance(b, int) and b == 0)
                behind = not (isinstance(b, int) and b <= 1)
                first, second = b * 2, b * 2 + 1

                def fill(u):
                    if shared:
                        unit(b - 1, u, b - 1)

                select_weights(first, 0)
                select_weights(second, 1)
                fill(0)
                rows(first, 0, b)
                fill(1)
                if shared:
                    positions(first - 2, 0)
                if not shared:
                    pe.wait_ge(s["consts"], 1)
                turn_rows(first, 0)
                fill(2)
                rows(second, 1, b)
                logits(first, 0)
                fill(3)
                if behind:
                    table_of(first - 3, 1)
                if shared:
                    positions(second - 2, 1)
                fill(4)
                turn_rows(second, 1)
                fill(5)
                logits(second, 1)
                if shared:
                    down(b - 1, second)
                    table_of(first - 2, 0)

            pe.wait_ge(s["tab3_done"], 3)
            body(0)
            pe.wait_ge(s["swlo_done"], 1)
            body(1)
            with pe.Fori(2, NB) as b:
                body(b)
            g = NB - 1
            unit(g, 0, g)
            positions(NG - 2, 0)
            unit(g, 1, g)
            unit(g, 2, g)
            unit(g, 3, g)
            positions(NG - 1, 1)
            unit(g, 4, g)
            unit(g, 5, g)
            unit(g + 1, 0, g + 1)
            table_of(NG - 3, 1)
            down(g, None)
            g = NB
            unit(g, 1, g)
            unit(g, 2, g)
            table_of(NG - 2, 0)
            unit(g, 3, g)
            table_of(NG - 1, 1)
            mm(tab_ps, zeros_h[:, :], zeros_h[:, 0:E], start=False, stop=True)
            mm(cnt_ps, ones[:, :], carry[:, NG, :], start=True, stop=True).then_inc(s["tab_final"], 1)
            unit(g, 4, g)
            unit(g, 5, g)

            def x_turn(e, slot):
                wait(pe, s["xlo_done"], e - 1)
                for k in range(KD):
                    last = nc.tensor.transpose(xeT_ps[slot % 2][:, k, :], xe[:, slot, k * P:(k + 1) * P], ident[:, :])
                last.then_inc(s["xt_done"], 1)

            def up(e, slot):
                pe.wait_ge(s["xlo_done"], e + 1)
                wait(pe, s["eh_done"], e - 1)
                n = 0
                i = slot % 2
                for k in range(KD):
                    pe.wait_ge(s["wlo_done"], e * KD + (k + 1))
                    for xt, wt in ((xeThi, w13hi), (xeThi, w13lo), (xeTlo, w13hi)):
                        last = mm(h_ps[i], xt[i][:, k, :], wt[i][:, k, :], start=(n == 0), stop=(n == 3 * KD - 1))
                        n += 1
                last.then_inc(s["h_done"], 1)

            def h_turn(e, slot):
                pe.wait_ge(s["eh_done"], e + 1)
                wait(pe, s["ehT_done"], e - 1)
                for k in range(2):
                    last = nc.tensor.transpose(ehT_ps[slot % 2][:, k, :], eh[:, slot % 2, k * IH:(k + 1) * IH], ident[:, :])
                last.then_inc(s["eht_done"], 1)

            def down_e(e, slot, rounds):
                pe.wait_ge(w2_in[slot], (rounds + 1) * 16)
                pe.wait_ge(s["ehT_done"], e + 1)
                wait(pe, s["eyrow_done"], e - 1)
                for k in range(2):
                    last = mm(ey_ps[slot % 2], ehT[0:IH, slot % 2, k, :], w2[:, slot, k, :], start=(k == 0), stop=(k == 1))
                last.then_inc(s["ey_done"], 1)

            def steady(e, slot, rounds_before, rounds_next):
                pe.wait_ge(xe_in[(slot + 1) % SLOTS], (rounds_next + 1) * 16)
                x_turn(e + 1, (slot + 1) % SLOTS)
                h_turn(e - 1, (slot - 1) % SLOTS)
                up(e, slot)
                down_e(e - 1, (slot - 1) % SLOTS, rounds_before)

            down_half(NB, 0, None)
            pe.wait_ge(s["hf_done"], EARLY * UNITS)
            pe.wait_ge(s["idx_done"], 1)
            for e in range(2):
                pe.wait_ge(xe_in[e], 16)
                x_turn(e, e)
            down_half(NB, 1, None)
            up(0, 0)
            pe.wait_ge(s["zadd_done"], EARLY * 2)
            for e in range(1, 1 + SLOTS):
                steady(e, e % SLOTS, (e - 1) // SLOTS, (e + 1) // SLOTS)
            with pe.Fori(1, (E - SLOTS) // SLOTS) as it:
                for j in range(SLOTS):
                    e = 1 + j
                    steady(it * SLOTS + e, e % SLOTS, it, it + (e + 1) // SLOTS)
            for e in range(E - SLOTS + 1, E - 1):
                steady(e, e % SLOTS, (e - 1) // SLOTS, (e + 1) // SLOTS)
            e = E - 1
            h_turn(e - 1, (e - 1) % SLOTS)
            up(e, e % SLOTS)
            down_e(e - 1, (e - 1) % SLOTS, E // SLOTS - 1)
            h_turn(e, e % SLOTS)
            down_e(e, e % SLOTS, E // SLOTS - 1)

            pe.wait_ge(s["eh_done"], E)
            pe.wait_ge(s["ehT_done"], E)
            unit(EARLY, 0, EARLY % YSLOTS)
            for g in LATE:
                for u in range(1, UNITS):
                    unit(g, u, g % YSLOTS)
                if g + 1 < NG:
                    unit(g + 1, 0, (g + 1) % YSLOTS)
                down(g, None)


def kernel(x, itok_B_0_7, fside_8xS_0, L0_cond_weights, L0_ffn_gate_w, L0_ffn_w1, L0_ffn_w2, L0_ffn_w3,
           L0_ffn_sw1, L0_ffn_sw2, L0_ffn_sw3):
    import concourse.bacc as bacc
    from concourse.bass_utils import run_bass_kernel_spmd

    w1, w3, w2 = np.asarray(L0_ffn_w1), np.asarray(L0_ffn_w3), np.asarray(L0_ffn_w2)
    up = np.concatenate([w1, w3], axis=1)
    lay = {
        "x": np.asarray(x),
        "subj": np.asarray(itok_B_0_7).reshape(1, B),
        "table": np.concatenate([np.asarray(L0_cond_weights), np.asarray(fside_8xS_0)[:, :, None]], axis=2).reshape(NSUB * C, CW),
        "gate_t": np.asarray(L0_ffn_gate_w).T.reshape(KD, P, E).transpose(1, 0, 2),
        "w13_t": up.transpose(0, 2, 1).reshape(E, KD, P, 2 * INTER).transpose(0, 2, 1, 3),
        "w2_t": w2.transpose(0, 2, 1).reshape(E, 2, IH, D).transpose(0, 2, 1, 3),
        "sw13_t": np.concatenate([np.asarray(L0_ffn_sw1), np.asarray(L0_ffn_sw3)], axis=0).T.reshape(KD, P, 2 * SINTER).transpose(1, 0, 2),
        "sw2_t": np.asarray(L0_ffn_sw2).T,
    }
    nc = bacc.Bacc("TRN2", target_bir_lowering=False, num_devices=1)
    arrays, aps = {}, {}
    for name, a in lay.items():
        a = np.ascontiguousarray(a)
        arrays[name] = a
        aps[name] = nc.dram_tensor(name, a.shape, mybir.dt.from_np(a.dtype), kind="ExternalInput").ap()
    aps["out"] = nc.dram_tensor("out", (B, C, T), F32, kind="ExternalOutput").ap()
    build_adaln_moe(nc, **aps)
    r = run_bass_kernel_spmd(nc, [arrays], core_ids=[0])
    return r.results[0]["out"]
```
